# Optimizing a Trainium2 kernel written in Bass

```python
import numpy as np
import jax
import jax.numpy as jnp

def _softmax(x, axis=-1):
    return jax.nn.softmax(x, axis=axis)

def _gelu(x):
    return jax.nn.gelu(x, approximate=True)

def _silu(x):
    return jax.nn.silu(x)

def _sigmoid(x):
    return jax.nn.sigmoid(x)

def _layernorm(x, axis=-1, eps=1e-05):
    m = jnp.mean(x, axis=axis, keepdims=True)
    v = jnp.var(x, axis=axis, keepdims=True)
    return (x - m) / jnp.sqrt(v + eps)

def _scatter_add(tgt, idx, src, axis=0):
    return tgt.at[idx].add(src)

def _segment_sum(src, seg, n):
    return jax.ops.segment_sum(src, seg, n)
kernel_name = 'mk_adj_preln_d2_adj_r2_b61508'

def setup_inputs(seed: int=0):
    np.random.seed(seed)
    _w = jnp.asarray

    def _rec_inputs():
        import jax
        import jax.numpy as jnp
        _gk = jax.random.key(seed)
        x = -0.0003929 + 0.9999 * jax.random.normal(jax.random.fold_in(_gk, 1), (32, 256, 256), jnp.float32)
        _a = jax.random.bernoulli(jax.random.fold_in(_gk, 2), 0.0078125, (32, 256, 256))
        _a = jnp.logical_or(_a, jnp.eye(256, dtype=bool))
        _af = _a.astype(jnp.float32)
        _af = _af * jax.random.uniform(jax.random.fold_in(_gk, 3), (32, 256, 256), jnp.float32, 0.05, 1)
        adj = _af
        return (x, adj)
    x, adj = _rec_inputs()

    def _L0_gnn_setup():
        import jax, jax.numpy as jnp
        import numpy as np
        EPS = 1e-06
        key = jax.random.key(seed)
        k1, k2, k3 = jax.random.split(key, 3)
        B, N, F, O = (8, 2048, 256, 256)
        x = jax.random.normal(k1, (B, N, F), dtype=jnp.float32)
        adj = jax.random.uniform(k2, (B, N, N), dtype=jnp.float32)
        W = jax.random.normal(k3, (O, 2 * F), dtype=jnp.float32) * (1.0 / np.sqrt(2 * F))
        return {'x': x, 'adj': adj, 'W': W}
    _L0_gnn_all = _L0_gnn_setup()
    _L0_gnn_in = {k: v for k, v in _L0_gnn_all.items() if k in ('W',)}
    del _L0_gnn_all

    def _L1_gnn_setup():
        import jax, jax.numpy as jnp
        import numpy as np
        EMBED_DIM = 256
        NUM_HEADS = 8
        HEAD_DIM = EMBED_DIM // NUM_HEADS
        SCALE = HEAD_DIM ** (-0.5)
        B, S = (16, 512)
        key = jax.random.key(seed)
        ks = jax.random.split(key, 12)
        init = lambda k, shape: jax.random.normal(k, shape, dtype=jnp.float32) * EMBED_DIM ** (-0.5)
        return {'x': jax.random.normal(ks[0], (B, S, EMBED_DIM), dtype=jnp.float32), 'adj_matrix': jax.random.uniform(ks[1], (B, S, S), dtype=jnp.float32), 'bond_matrix': jax.random.uniform(ks[2], (B, S, S), dtype=jnp.float32), 'Wq': init(ks[3], (EMBED_DIM, EMBED_DIM)), 'bq': jnp.zeros((EMBED_DIM,), jnp.float32), 'Wk': init(ks[4], (EMBED_DIM, EMBED_DIM)), 'bk': jnp.zeros((EMBED_DIM,), jnp.float32), 'Wv': init(ks[5], (EMBED_DIM, EMBED_DIM)), 'bv': jnp.zeros((EMBED_DIM,), jnp.float32), 'Wo': init(ks[6], (EMBED_DIM, EMBED_DIM)), 'bo': jnp.zeros((EMBED_DIM,), jnp.float32), 'seq_len': S}
    _L1_gnn_all = _L1_gnn_setup()
    _L1_gnn_in = {k: v for k, v in _L1_gnn_all.items() if k in ('Wq', 'bq', 'Wk', 'bk', 'Wv', 'bv', 'Wo', 'bo')}
    del _L1_gnn_all
    return {'x': x, 'adj': adj, 'L0_gnn_W': _L0_gnn_in['W'], 'L1_gnn_Wq': _L1_gnn_in['Wq'], 'L1_gnn_bq': _L1_gnn_in['bq'], 'L1_gnn_Wk': _L1_gnn_in['Wk'], 'L1_gnn_bk': _L1_gnn_in['bk'], 'L1_gnn_Wv': _L1_gnn_in['Wv'], 'L1_gnn_bv': _L1_gnn_in['bv'], 'L1_gnn_Wo': _L1_gnn_in['Wo'], 'L1_gnn_bo': _L1_gnn_in['bo']}

def reference(x, adj, L0_gnn_W, L1_gnn_Wq, L1_gnn_bq, L1_gnn_Wk, L1_gnn_bk, L1_gnn_Wv, L1_gnn_bv, L1_gnn_Wo, L1_gnn_bo):
    import jax
    import jax.numpy as jnp

    def _L0_gnn_ref(x, adj, W):
        import jax, jax.numpy as jnp
        import numpy as np
        EPS = 1e-06
        deg = jnp.sum(adj, axis=-1, keepdims=True)
        agg = jnp.einsum('bij,bjf->bif', adj, x) / jnp.maximum(deg, EPS)
        cat = jnp.concatenate([x, agg], axis=2)
        out = jnp.einsum('bnf,of->bno', cat, W)
        return jax.nn.relu(out)

    def _L1_gnn_ref(x, adj_matrix, bond_matrix, Wq, bq, Wk, bk, Wv, bv, Wo, bo, seq_len):
        import jax, jax.numpy as jnp
        import numpy as np
        EMBED_DIM = 256
        NUM_HEADS = 8
        HEAD_DIM = EMBED_DIM // NUM_HEADS
        SCALE = HEAD_DIM ** (-0.5)
        B, S = (16, 512)
        b = x.shape[0]

        def proj(W, bias):
            y = jnp.einsum('bse,fe->bsf', x, W) + bias
            return y.reshape(b, seq_len, NUM_HEADS, HEAD_DIM).transpose(0, 2, 1, 3)
        q, k, v = (proj(Wq, bq), proj(Wk, bk), proj(Wv, bv))
        scores = jnp.einsum('bhqd,bhkd->bhqk', q, k) * SCALE
        mask = (adj_matrix + bond_matrix)[:, None, :, :]
        scores = scores * mask
        attn = jax.nn.softmax(scores, axis=-1)
        ctx = jnp.einsum('bhqk,bhkd->bhqd', attn, v)
        ctx = ctx.transpose(0, 2, 1, 3).reshape(b, seq_len, EMBED_DIM)
        return jnp.einsum('bse,fe->bsf', ctx, Wo) + bo
    h = jnp.maximum(_layernorm(x, axis=-1), 0.0)
    x = x + _L0_gnn_ref(h, adj, L0_gnn_W)
    h = jnp.maximum(_layernorm(x, axis=-1), 0.0)
    x = x + _L1_gnn_ref(h, adj, adj, L1_gnn_Wq, L1_gnn_bq, L1_gnn_Wk, L1_gnn_bk, L1_gnn_Wv, L1_gnn_bv, L1_gnn_Wo, L1_gnn_bo, 256)
    return x

_drawn_inputs = setup_inputs


def setup_inputs(seed=0):
    import zlib

    import numpy as np

    out = dict(_drawn_inputs(seed))
    spreads = {'L1_gnn_bq': (0.0, 0.8),
     'L1_gnn_bk': (0.0, 0.8),
     'L1_gnn_bv': (0.0, 0.1),
     'L1_gnn_bo': (0.0, 0.1)}
    factors = {'L1_gnn_Wq': 8.0, 'L1_gnn_Wk': 8.0}
    for name, (base, spread) in spreads.items():
        noise = np.random.default_rng([zlib.crc32(name.encode()), seed]).standard_normal(out[name].shape)
        drawn = base * np.exp(spread * noise) if base else spread * noise
        out[name] = jnp.asarray(drawn.astype(out[name].dtype))
    for name, factor in factors.items():
        out[name] = (out[name] * factor).astype(out[name].dtype)
    return out
```

```python
from contextlib import ExitStack

import concourse.bass as bass
from concourse import mybir

ALU = mybir.AluOpType
ACT = mybir.ActivationFunctionType
F32 = mybir.dt.float32
F32R = mybir.dt.float32r

P = 128
N = 256
F = 256
T = N // P
H = 8
D = F // H
G = P // D
LN_EPS = 1e-5
DEG_EPS = 1e-6
SCALE2 = 2.0 * float(D) ** -0.5
LOWEST = -3.0e38

PARTS = ((0, 0), (0, 1), (1, 0))

K_LO, K_HI, Q_HI, Q_LO = range(4)
STACK = ((K_HI, Q_HI), (K_LO, Q_HI), (K_HI, Q_LO))
STACK_ROWS = D * len(STACK)
STACK_INC = 16 * len(STACK)



def shifted(i, by):
    return (i[0], i[1] + by)


def wait_count(eng, sem, i, per=1, more=0):
    j, c = i
    fixed = per * c + more
    if isinstance(j, int):
        if fixed > 0:
            eng.wait_ge(sem, fixed)
    else:
        eng.wait_ge(sem, j * (2 * per) + fixed)


def wait_dma(eng, sems, i, inc=16):
    j, c = i
    sem, fixed = sems[c % 2], inc * (c // 2 + 1)
    if isinstance(j, int):
        if fixed > 0:
            eng.wait_ge(sem, fixed)
    else:
        eng.wait_ge(sem, j * inc + fixed)


def pass_waits(eng, s_passed):
    eng.sem_inc(s_passed, 1)


def batch_of(dram, i):
    return dram[i[0] * 2 + i[1]]


def build(nc, x, adjq, adjt, w0, wq, wk, wv, wo, bq, bk, bv, bo, out):
    B = x.shape[0]
    assert B % 2 == 0 and B >= 8 and N == 2 * P and F == 2 * P

    with ExitStack() as ctx:
        def sb(name, shape, dt=F32):
            return ctx.enter_context(nc.sbuf_tensor(name, shape, dt))

        def ps(name):
            return ctx.enter_context(nc.psum_tensor(name, [P, T, 256], F32))

        def sem(name):
            return ctx.enter_context(nc.semaphore(name))

        def sems(name):
            return [sem(f"{name}_of_parity{p}") for p in range(2)]

        w_raw = sb("w_raw", [P, 12, 256])
        w_hi, w_lo = sb("w_hi", [P, 12, 256], F32R), sb("w_lo", [P, 12, 256], F32R)
        W = (w_hi, w_lo)
        W0, WQ, WK, WV, WO = 0, 4, 6, 8, 10
        bq_sb, bk_sb, bv_sb = (sb(n, [P, T]) for n in ("bq_sb", "bk_sb", "bv_sb"))
        bv_wide = sb("bv_wide", [P, T, P])
        bo_row = sb("bo_row", [1, F])
        ones_row = sb("ones_row", [1, P])
        out_bias = sb("out_bias", [P, F])
        ident = sb("ident", [P, P])
        minus_half = sb("minus_half", [P, T])

        x_sb = [sb(f"x_sb{p}", [P, T, F]) for p in range(2)]
        adjt_sb = [sb(f"adjt_sb{p}", [P, T, N]) for p in range(2)]
        adjq_sb = [sb(f"adjq_sb{p}", [P, T, N]) for p in range(2)]
        mask = [sb(f"mask{p}", [P, T, N]) for p in range(2)]
        stats1, stats2 = sb("stats1", [P, T, 6]), sb("stats2", [P, T, 6])
        mv1, mv2 = sb("mv1", [P, T, 2]), sb("mv2", [P, T, 2])
        var1, var2 = sb("var1", [P, T]), sb("var2", [P, T])
        rstd1, rstd2 = sb("rstd1", [P, T]), sb("rstd2", [P, T])
        y1, y2 = sb("y1", [P, T, F]), sb("y2", [P, T, F])
        h1 = (sb("h1_hi", [P, T, F], F32R), sb("h1_lo", [P, T, F], F32R))
        at = (sb("at_hi", [P, T, N], F32R), sb("at_lo", [P, T, N], F32R))
        h1t = (sb("h1t_hi", [P, T, N], F32R), sb("h1t_lo", [P, T, N], F32R))
        aggt = (sb("aggt_hi", [P, T, N], F32R), sb("aggt_lo", [P, T, N], F32R))
        deg_junk = sb("deg_junk", [P, T, N])
        deg, deg_max, deg_inv = sb("deg", [P, T]), sb("deg_max", [P, T]), sb("deg_inv", [P, T])
        self_part = sb("self_part", [P, T, F])
        l0_sum = sb("l0_sum", [P, T, F])
        x1 = [sb(f"x1_{p}", [P, T, F]) for p in range(2)]
        x1_biased = [sb(f"x1_biased{p}", [P, T, F]) for p in range(2)]
        h2t = (sb("h2t_hi", [P, T, N], F32R), sb("h2t_lo", [P, T, N], F32R))
        kq = sb("kq", [P, 4, T, N], F32R)
        kq_stack = [sb(f"kq_stack{p}", [STACK_ROWS, G, 2, T, N], F32R) for p in range(2)]
        v_sb = [sb(f"v_sb{p}", [P, T, F]) for p in range(2)]
        masked = [sb(f"masked{p}", [P, T, N]) for p in range(2)]
        row_max, neg_max = sb("row_max", [P, 2, T]), sb("neg_max", [P, 2, T])
        row_sum, inv_sum = sb("row_sum", [P, 2, T]), sb("inv_sum", [P, 2, T])
        probs = [sb(f"probs{p}", [P, T, N]) for p in range(2)]
        attn = [sb(f"attn{p}", [P, T, N]) for p in range(2)]
        attn_t = sb("attn_t", [P, H, T, N])
        ctxt = (sb("ctxt_hi", [P, T, N], F32R), sb("ctxt_lo", [P, T, N], F32R))
        out_sb = [sb(f"out_sb{p}", [P, T, F]) for p in range(2)]

        ps_s = [ps("ps_s0"), ps("ps_s1")]
        ps_t = [ps("ps_t0"), ps("ps_t1")]
        ps_ctx = ps("ps_ctx")
        ps_x, ps_y, ps_z = ps("ps_x"), ps("ps_y"), ps("ps_z")

        s_weights = sem("s_weights")
        s_x, s_adjt, s_adjq, s_mask = sems("s_x"), sems("s_adjt"), sems("s_adjq"), sems("s_mask")
        s_stored = sems("s_stored")
        s_stack = [sems(f"s_stack_head{g}") for g in range(G)]
        s_passed = sem("s_passed")
        s_ident = sem("s_ident")
        s_consts = sem("s_consts")
        s_w_hi, s_w_lo = sem("s_w_hi"), sem("s_w_lo")
        s_bv_wide, s_bias_ready, s_bias_copied = sem("s_bv_wide"), sem("s_bias_ready"), sem("s_bias_copied")
        s_scores = sem("s_scores")
        s_masked = sem("s_masked")
        s_negmax = sem("s_negmax")
        s_exp = sem("s_exp")
        s_inv = sem("s_inv")
        s_attn = sem("s_attn")
        s_attn_t = sem("s_attn_t")
        s_attn_copied = sem("s_attn_copied")
        s_ctx_half, s_ctx = sem("s_ctx_half"), sem("s_ctx")
        s_ctx_hi, s_ctx_lo = sem("s_ctx_hi"), sem("s_ctx_lo")
        s_out, s_added = sem("s_out"), sem("s_added")
        s_stats1, s_mv1, s_var1 = sem("s_stats1"), sem("s_mv1"), sem("s_var1")
        s_rstd1, s_y1 = sem("s_rstd1"), sem("s_y1")
        s_h1_hi, s_h1_lo = sem("s_h1_hi"), sem("s_h1_lo")
        s_at_hi, s_at_lo = sem("s_at_hi"), sem("s_at_lo")
        s_y1t, s_h1t_hi, s_h1t_lo = sem("s_y1t"), sem("s_h1t_hi"), sem("s_h1t_lo")
        s_agg, s_agg_hi, s_agg_lo = sem("s_agg"), sem("s_agg_hi"), sem("s_agg_lo")
        s_self, s_self_copied = sem("s_self"), sem("s_self_copied")
        s_nbr = sem("s_nbr")
        s_deg, s_deg_max, s_deg_inv = sem("s_deg"), sem("s_deg_max"), sem("s_deg_inv")
        s_l0_sum, s_x1 = sem("s_l0_sum"), sem("s_x1")
        s_stats2, s_mv2, s_var2 = sem("s_stats2"), sem("s_mv2"), sem("s_var2")
        s_rstd2, s_y2 = sem("s_rstd2"), sem("s_y2")
        s_x1_biased = sem("s_x1_biased")
        s_y2t, s_h2t_hi, s_h2t_lo = sem("s_y2t"), sem("s_h2t_hi"), sem("s_h2t_lo")
        s_q, s_q_hi, s_q_lo = sem("s_q"), sem("s_q_hi"), sem("s_q_lo")
        s_k, s_k_hi, s_k_lo = sem("s_k"), sem("s_k_hi"), sem("s_k_lo")
        s_v, s_v_copied = sem("s_v"), sem("s_v_copied")

        block = ctx.enter_context(nc.Block())

        def there(i, by=0):
            return not isinstance(i[0], int) or 0 <= i[1] + by < B

        def at_start(i, c):
            return isinstance(i[0], int) and i[1] == c

        def head_there(i, g):
            return there(i, g // H)

        def run(eng, iteration):
            for c in range(-3, 2):
                iteration((0, c))
            with eng.Fori(1, B // 2 - 2) as j:
                iteration((j, 0))
                iteration((j, 1))
            for c in range(B - 4, B + 1):
                iteration((0, c))

        @block.sync
        def _(sp):
            weights = ((w_raw[:, W0:W0 + 4, :], w0), (w_raw[:, WQ:WQ + 2, :], wq), (w_raw[:, WK:WK + 2, :], wk),
                       (w_raw[:, WV:WV + 2, :], wv), (w_raw[:, WO:WO + 2, :], wo),
                       (bq_sb[:, :], bq), (bk_sb[:, :], bk), (bv_sb[:, :], bv), (bo_row[:, :], bo))
            def iteration(i):
                c = i[1]
                b, nxt = shifted(i, 1), shifted(i, 3)
                if there(nxt):
                    wait_count(sp, s_x1, nxt, 1, -1)
                    sp.dma_start(x_sb[(c + 3) % 2][:, :, :], batch_of(x, nxt)).then_inc(s_x[(c + 3) % 2], 16)
                    wait_count(sp, s_at_lo, nxt, 1, -1)
                    sp.dma_start(adjt_sb[(c + 3) % 2][:, :, :], batch_of(adjt, nxt)).then_inc(s_adjt[(c + 3) % 2], 16)
                if at_start(i, -3):
                    for dst, src in weights:
                        sp.dma_start(dst, src).then_inc(s_weights, 16)
                if there(b):
                    wait_dma(sp, s_adjq, b)
                    pass_waits(sp, s_passed)
                    wait_count(sp, s_masked, i, H, 0)
                    sp.dma_start(mask[(c + 1) % 2][:, :, :], adjq_sb[(c + 1) % 2][:, :, :])\
                      .then_inc(s_mask[(c + 1) % 2], 16)
                if there(nxt):
                    if there(b):
                        wait_dma(sp, s_mask, b)
                    wait_count(sp, s_deg, nxt, 1, -1)
                    sp.dma_start(adjq_sb[(c + 3) % 2][:, :, :], batch_of(adjq, nxt)).then_inc(s_adjq[(c + 3) % 2], 16)
                if there(b):
                    wait_count(sp, s_scores, i, H, 0)
                    for s_part in (s_q_hi, s_q_lo, s_k_hi, s_k_lo):
                        wait_count(sp, s_part, b, 1, 1)
                    for g in range(G):
                        for r, (k_part, q_part) in enumerate(STACK):
                            sp.dma_start(kq_stack[(c + 1) % 2][D * r:D * r + D, g, :, :, :].bitcast(F32),
                                         kq[D * g:D * g + D, k_part:q_part + 1:q_part - k_part, :, :].bitcast(F32))\
                              .then_inc(s_stack[g][(c + 1) % 2], 16)
                if there(i, -1):
                    wait_count(sp, s_added, i, 1, 0)
                    sp.dma_start(batch_of(out, shifted(i, -1)), out_sb[(c - 1) % 2][:, :, :])\
                      .then_inc(s_stored[(c - 1) % 2], 16)
            run(sp, iteration)
            for p in range(2):
                sp.wait_ge(s_stored[p], 16 * (B // 2))

        @block.tensor
        def _(pe):
            mm = nc.tensor.matmul

            def product(dst, stationary, moving, first_s=0, first_m=0):
                for o in range(T):
                    for c in range(T):
                        for n, (a, b) in enumerate(PARTS):
                            last = mm(dst[:, o, :], stationary[a][:, first_s + c, o * P:o * P + P],
                                      moving[b][:, first_m + c, :],
                                      start=(c == 0 and n == 0), stop=(c == T - 1 and n == len(PARTS) - 1))
                return last

            def transposed(dst, src):
                for f in range(T):
                    for t in range(T):
                        last = nc.tensor.transpose(dst[:, f, t * P:t * P + P], src[:, t, f * P:f * P + P], ident[:, :])
                return last

            def scores(i, g):
                p, ft, j = (i[1] + g // H) % 2, g % H // G, g % G
                wait_count(pe, s_masked, i, H, g - 1)
                if ft == 0:
                    wait_dma(pe, s_stack[j], shifted(i, g // H), STACK_INC)
                for t in range(T):
                    last = mm(ps_s[g % 2][:, t, :], kq_stack[p][:, j, 1, ft, t * P:t * P + P], kq_stack[p][:, j, 0, ft, :],
                              start=True, stop=True)
                last.then_inc(s_scores, 1)

            def attn_transposed(i, g):
                wait_count(pe, s_attn, i, H, g + 1)
                wait_count(pe, s_attn_copied, i, H, g - 1)
                transposed(ps_t[g % 2], attn[g % 2]).then_inc(s_attn_t, 1)

            def context(i, ft):
                for c in range(T):
                    for j in range(G):
                        h = G * ft + j
                        last = mm(ps_ctx[D * j:D * j + D, ft, :], v_sb[i[1] % 2][:, c, D * h:D * h + D],
                                  attn_t[:, h, c, :], start=(c == 0), stop=(c == T - 1))
                return last

            pe.wait_ge(s_ident, 2)
            pe.wait_ge(s_consts, 2)
            pe.wait_ge(s_weights, 16 * 9)
            pe.wait_ge(s_bv_wide, 1)
            for c in range(T):
                mm(ps_ctx[:, 0, :], bv_wide[:, c, :], w_raw[:, WO + c, :], start=(c == 0), stop=False)
            mm(ps_ctx[:, 0, :], ones_row[:, :], bo_row[:, :], start=False, stop=True).then_inc(s_bias_ready, 1)
            pe.wait_ge(s_w_hi, 1)
            pe.wait_ge(s_w_lo, 1)

            def iteration(i):
                a, b = shifted(i, 2), shifted(i, 1)
                fa, fb, att, done = there(a), there(b), there(i), there(i, -1)
                for g in range(H):
                    if head_there(i, g + 1):
                        scores(i, g + 1)
                    if g == 0 and fa:
                        wait_count(pe, s_y1, a, 1, 1)
                        wait_count(pe, s_self_copied, a, 1, 0)
                        transposed(ps_x, y1).then_inc(s_y1t, 1)
                        wait_count(pe, s_h1_hi, a, 1, 1)
                        wait_count(pe, s_h1_lo, a, 1, 1)
                        wait_count(pe, s_at_hi, a, 1, 1)
                        wait_count(pe, s_at_lo, a, 1, 1)
                        wait_count(pe, s_l0_sum, a, 1, 0)
                        product(ps_y, h1, at).then_inc(s_agg, 1)
                    if g == 1 and fb:
                        wait_count(pe, s_y2, b, 1, 1)
                        wait_count(pe, s_v_copied, b, 1, 0)
                        transposed(ps_z, y2).then_inc(s_y2t, 1)
                    if g == 1 and done:
                        wait_count(pe, s_attn_copied, i, H, 0)
                        context(shifted(i, -1), 1).then_inc(s_ctx, 1)
                    if g == 2 and fb:
                        wait_count(pe, s_h2t_lo, b, 1, 1)
                        if fa:
                            wait_count(pe, s_h1t_lo, a, 1, 1)
                        else:
                            wait_count(pe, s_self_copied, a, 1, 0)
                        product(ps_x, W, h2t, first_s=WQ).then_inc(s_q, 1)
                    if g == 3 and fb:
                        if fa:
                            wait_count(pe, s_agg_lo, a, 1, 1)
                        else:
                            wait_count(pe, s_l0_sum, a, 1, 0)
                        product(ps_y, W, h2t, first_s=WK).then_inc(s_k, 1)
                    if g == 4 and done:
                        wait_count(pe, s_ctx_lo, i, 1, 0)
                        if fb:
                            wait_count(pe, s_h2t_lo, b, 1, 1)
                        elif att:
                            wait_count(pe, s_v_copied, b, 1, 0)
                        else:
                            wait_count(pe, s_added, i, 1, -1)
                        product(ps_z, ctxt, W, first_m=WO).then_inc(s_out, 1)
                    if g == 5 and att:
                        wait_count(pe, s_attn_copied, i, H, G)
                        wait_count(pe, s_v_copied, i, 1, 1)
                        wait_count(pe, s_ctx_lo, i, 1, 0)
                        if at_start(i, 0):
                            pe.wait_ge(s_bias_copied, 1)
                        context(i, 0).then_inc(s_ctx_half, 1)
                    if g == 5 and fa:
                        wait_count(pe, s_h1t_lo, a, 1, 1)
                        if fb:
                            wait_count(pe, s_q_lo, b, 1, 1)
                        product(ps_x, h1t, W, first_m=W0).then_inc(s_self, 1)
                    if g == 6 and fa:
                        wait_count(pe, s_agg_lo, a, 1, 1)
                        if fb:
                            wait_count(pe, s_k_lo, b, 1, 1)
                        product(ps_y, aggt, W, first_m=W0 + T).then_inc(s_nbr, 1)
                    if g == 7 and fb:
                        if done:
                            wait_count(pe, s_added, i, 1, 0)
                        product(ps_z, h2t, W, first_m=WV).then_inc(s_v, 1)
                    if head_there(i, g - 1):
                        attn_transposed(i, g - 1)
            run(pe, iteration)

        @block.scalar
        def _(act):
            copy = ACT.Copy

            act.wait_ge(s_bias_ready, 1)
            nc.scalar.activation(out_bias[:, :], ps_ctx[:, 0, :], copy).then_inc(s_bias_copied, 1)

            def exponentials(i, g):
                p = g % 2
                wait_count(act, s_negmax, i, H, g + 1)
                wait_count(act, s_attn, i, H, g - 1)
                for t in range(T):
                    last = nc.scalar.activation(probs[p][:, t, :], masked[p][:, t, :], ACT.Exp,
                                                bias=neg_max[:, p, t:t + 1], scale=SCALE2,
                                                accum_out=row_sum[:, p, t:t + 1])
                last.then_inc(s_exp, 1)

            def attn_copy(i, g):
                wait_count(act, s_attn_t, i, H, g + 1)
                used = shifted(i, g // H)
                wait_count(act, s_ctx if g % H >= G else s_ctx_half, used, 1, 0)
                nc.scalar.activation(attn_t[:, g % H, :, :], ps_t[g % 2][:, :, :], copy).then_inc(s_attn_copied, 1)

            def iteration(i):
                a, b, n = shifted(i, 2), shifted(i, 1), shifted(i, 3)
                fa, fb, fn, att, done = there(a), there(b), there(n), there(i), there(i, -1)
                for g in range(H):
                    if att:
                        exponentials(i, g)
                    if g == 0 and att:
                        wait_count(act, s_v, i, 1, 1)
                        wait_count(act, s_ctx, i, 1, -1)
                        nc.scalar.activation(v_sb[i[1] % 2][:, :, :], ps_z[:, :, :], copy).then_inc(s_v_copied, 1)
                    if g == 0 and fa:
                        wait_count(act, s_y1t, a, 1, 1)
                        wait_count(act, s_self, a, 1, 0)
                        nc.scalar.activation(h1t[0][:, :, :], ps_x[:, :, :], ACT.Relu).then_inc(s_h1t_hi, 1)
                    if g == 1 and fa:
                        wait_count(act, s_agg, a, 1, 1)
                        wait_count(act, s_nbr, a, 1, 0)
                        nc.scalar.activation(aggt[0][:, :, :], ps_y[:, :, :], copy).then_inc(s_agg_hi, 1)
                    if g == 1 and fb:
                        wait_count(act, s_y2t, b, 1, 1)
                        wait_count(act, s_v, b, 1, 0)
                        nc.scalar.activation(h2t[0][:, :, :], ps_z[:, :, :], ACT.Relu).then_inc(s_h2t_hi, 1)
                    if g == 2 and done:
                        wait_count(act, s_ctx, i, 1, 0)
                        wait_count(act, s_out, i, 1, -1)
                        nc.scalar.activation(ctxt[0][:, :, :], ps_ctx[:, :, :], copy).then_inc(s_ctx_hi, 1)
                    if g in (3, 4) and fb:
                        s_ready, bank, bias, part, s_done = (
                            (s_q, ps_x, bq_sb, Q_HI, s_q_hi) if g == 3 else (s_k, ps_y, bk_sb, K_HI, s_k_hi))
                        wait_count(act, s_ready, b, 1, 1)
                        if g == 3:
                            for head in range(G):
                                wait_dma(act, s_stack[head], i, STACK_INC)
                        for f in range(T):
                            last = nc.scalar.activation(kq[:, part, f, :], bank[:, f, :], ACT.Identity, bias=bias[:, f:f + 1])
                        last.then_inc(s_done, 1)
                    if g == 5 and fa:
                        wait_dma(act, s_adjq, a)
                        wait_count(act, s_deg_max, a, 1, 0)
                        for t in range(T):
                            last = nc.scalar.activation(deg_junk[:, t, :], adjq_sb[i[1] % 2][:, t, :], copy,
                                                        accum_out=deg[:, t:t + 1])
                        last.then_inc(s_deg, 1)
                    if g == 6 and fa:
                        wait_count(act, s_self, a, 1, 1)
                        wait_count(act, s_l0_sum, a, 1, 0)
                        nc.scalar.activation(self_part[:, :, :], ps_x[:, :, :], copy).then_inc(s_self_copied, 1)
                    if g == 6 and fn:
                        wait_count(act, s_y1, n, 1, 1)
                        wait_count(act, s_agg, n, 1, 0)
                        nc.scalar.activation(h1[0][:, :, :], y1[:, :, :], ACT.Relu).then_inc(s_h1_hi, 1)
                    if head_there(i, g - 1):
                        attn_copy(i, g - 1)
            run(act, iteration)

        @block.vector
        def _(dve):
            v = nc.vector
            f32 = lambda ap: ap.bitcast(F32)

            def split_weights():
                dve.wait_ge(s_weights, 16 * 9)
                v.tensor_copy(bv_wide[:, :, :], bv_sb[:, :].unsqueeze(2).to_broadcast([P, T, P])).then_inc(s_bv_wide, 1)
                v.tensor_copy(w_hi[:, :, :], w_raw[:, :, :]).then_inc(s_w_hi, 1)
                dve.wait_ge(s_w_hi, 1)
                v.tensor_tensor(w_lo[:, :, :], w_raw[:, :, :], f32(w_hi[:, :, :]), ALU.subtract).then_inc(s_w_lo, 1)

            def variances(i, src, stats, mv, var, s_stats, s_mv, s_var):
                for t in range(T):
                    last = v.bn_stats(stats[:, t, :], src[:, t, :])
                last.then_inc(s_stats, 1)
                wait_count(dve, s_stats, i, 1, 1)
                pass_waits(dve, s_passed)
                for t in range(T):
                    last = v.bn_aggr(mv[:, t, :], stats[:, t, :])
                last.then_inc(s_mv, 1)
                wait_count(dve, s_mv, i, 1, 1)
                v.tensor_scalar(var[:, :], mv[:, :, 1], LN_EPS, None, ALU.add).then_inc(s_var, 1)

            def normalised(dst, src, mv, rstd):
                for t in range(T):
                    last = v.tensor_scalar(dst[:, t, :], src[:, t, :], mv[:, t, 0:1], rstd[:, t:t + 1],
                                           ALU.subtract, ALU.mult)
                return last

            def masked_scores(i, g):
                p, m = g % 2, (i[1] + g // H) % 2
                wait_count(dve, s_scores, i, H, g + 1)
                wait_count(dve, s_exp, i, H, g - 1)
                if g == H:
                    wait_dma(dve, s_mask, shifted(i, 1))
                pass_waits(dve, s_passed)
                for t in range(T):
                    last = v.tensor_tensor_reduce(out=masked[p][:, t, :], in0=ps_s[p][:, t, :], in1=mask[m][:, t, :],
                                                  scale=1.0, scalar=LOWEST, op0=ALU.mult, op1=ALU.max,
                                                  accum_out=row_max[:, p, t:t + 1])
                last.then_inc(s_masked, 1)
                wait_count(dve, s_masked, i, H, g + 1)
                v.tensor_scalar(neg_max[:, p, :], row_max[:, p, :], -SCALE2, None, ALU.mult).then_inc(s_negmax, 1)

            def inverse_sums(i, g):
                p = g % 2
                wait_count(dve, s_exp, i, H, g + 1)
                wait_count(dve, s_attn, i, H, g - 1)
                v.reciprocal(inv_sum[:, p, :], row_sum[:, p, :]).then_inc(s_inv, 1)

            def iteration(i):
                a, b, n = shifted(i, 2), shifted(i, 1), shifted(i, 3)
                fa, fb, fn, att, done = there(a), there(b), there(n), there(i), there(i, -1)
                for g in range(H):
                    if head_there(i, g + 1):
                        masked_scores(i, g + 1)
                    if att:
                        inverse_sums(i, g)
                    if g == 0 and fb:
                        wait_count(dve, s_rstd2, b, 1, 1)
                        wait_count(dve, s_y2t, b, 1, 0)
                        normalised(y2, x1[(i[1] + 1) % 2], mv2, rstd2).then_inc(s_y2, 1)
                    if g == 0 and fa:
                        wait_count(dve, s_h1t_hi, a, 1, 1)
                        v.scalar_tensor_tensor(h1t[1][:, :, :], ps_x[:, :, :], 0.0, f32(h1t[0][:, :, :]),
                                               ALU.max, ALU.subtract).then_inc(s_h1t_lo, 1)
                    if g == 1 and fa:
                        wait_count(dve, s_agg_hi, a, 1, 1)
                        v.tensor_tensor(aggt[1][:, :, :], ps_y[:, :, :], f32(aggt[0][:, :, :]), ALU.subtract)\
                         .then_inc(s_agg_lo, 1)
                    if g == 1 and fb:
                        wait_count(dve, s_h2t_hi, b, 1, 1)
                        v.scalar_tensor_tensor(h2t[1][:, :, :], ps_z[:, :, :], 0.0, f32(h2t[0][:, :, :]),
                                               ALU.max, ALU.subtract).then_inc(s_h2t_lo, 1)
                    if g == 2 and done:
                        wait_count(dve, s_ctx_hi, i, 1, 0)
                        v.tensor_tensor(ctxt[1][:, :, :], ps_ctx[:, :, :], f32(ctxt[0][:, :, :]), ALU.subtract)\
                         .then_inc(s_ctx_lo, 1)
                    if g in (3, 4) and fb:
                        s_hi, bank, bias, hi, lo, s_done = (
                            (s_q_hi, ps_x, bq_sb, Q_HI, Q_LO, s_q_lo) if g == 3 else
                            (s_k_hi, ps_y, bk_sb, K_HI, K_LO, s_k_lo))
                        wait_count(dve, s_hi, b, 1, 1)
                        for f in range(T):
                            last = v.scalar_tensor_tensor(kq[:, lo, f, :], bank[:, f, :], bias[:, f:f + 1],
                                                          f32(kq[:, hi, f, :]), ALU.add, ALU.subtract)
                        last.then_inc(s_done, 1)
                    if g == 4 and fn:
                        wait_dma(dve, s_x, n)
                        wait_count(dve, s_rstd1, n, 1, 0)
                        variances(n, x_sb[(i[1] + 1) % 2], stats1, mv1, var1, s_stats1, s_mv1, s_var1)
                    if g == 5 and done:
                        wait_count(dve, s_out, i, 1, 0)
                        wait_count(dve, s_x1_biased, i, 1, 0)
                        wait_dma(dve, s_stored, shifted(i, -3))
                        v.tensor_tensor(out_sb[(i[1] - 1) % 2][:, :, :], ps_z[:, :, :],
                                        x1_biased[(i[1] - 1) % 2][:, :, :], ALU.add).then_inc(s_added, 1)
                    if g == 5 and fn:
                        wait_count(dve, s_rstd1, n, 1, 1)
                        wait_count(dve, s_y1t, n, 1, 0)
                        wait_count(dve, s_h1_lo, n, 1, 0)
                        normalised(y1, x_sb[(i[1] + 1) % 2], mv1, rstd1).then_inc(s_y1, 1)
                    if g == 6 and fn:
                        wait_count(dve, s_agg, n, 1, 0)
                        wait_dma(dve, s_adjt, n)
                        v.tensor_copy(at[0][:, :, :], adjt_sb[(i[1] + 1) % 2][:, :, :]).then_inc(s_at_hi, 1)
                        wait_count(dve, s_h1_hi, n, 1, 1)
                        v.scalar_tensor_tensor(h1[1][:, :, :], y1[:, :, :], 0.0, f32(h1[0][:, :, :]),
                                               ALU.max, ALU.subtract).then_inc(s_h1_lo, 1)
                    if g == 7 and fa:
                        wait_count(dve, s_deg, a, 1, 1)
                        v.tensor_scalar(deg_max[:, :], deg[:, :], DEG_EPS, None, ALU.max).then_inc(s_deg_max, 1)
                        wait_count(dve, s_deg_max, a, 1, 1)
                        v.reciprocal(deg_inv[:, :], deg_max[:, :]).then_inc(s_deg_inv, 1)
                        wait_count(dve, s_deg_inv, a, 1, 1)
                        wait_count(dve, s_nbr, a, 1, 1)
                        wait_count(dve, s_self_copied, a, 1, 1)
                        for t in range(T):
                            last = v.scalar_tensor_tensor(l0_sum[:, t, :], ps_y[:, t, :], deg_inv[:, t:t + 1],
                                                          self_part[:, t, :], ALU.mult, ALU.add)
                        last.then_inc(s_l0_sum, 1)
                        wait_count(dve, s_l0_sum, a, 1, 1)
                        wait_count(dve, s_x1_biased, a, 1, -1)
                        v.scalar_tensor_tensor(x1[i[1] % 2][:, :, :], l0_sum[:, :, :], 0.0, x_sb[i[1] % 2][:, :, :],
                                               ALU.max, ALU.add).then_inc(s_x1, 1)
                        wait_count(dve, s_x1, a, 1, 1)
                        wait_count(dve, s_rstd2, a, 1, 0)
                        wait_count(dve, s_y2, a, 1, 0)
                        variances(a, x1[i[1] % 2], stats2, mv2, var2, s_stats2, s_mv2, s_var2)
                    if g == 0 and at_start(i, -3):
                        split_weights()
            run(dve, iteration)

        @block.gpsimd
        def _(pool):
            gp = nc.gpsimd
            gp.memset(ident[:, :], 0.0).then_inc(s_ident, 1)
            gp.memset(ones_row[:, :], 1.0).then_inc(s_consts, 1)
            gp.memset(minus_half[:, :], -0.5).then_inc(s_consts, 1)
            pool.wait_ge(s_ident, 1)
            gp.affine_select(out=ident[:, :], in_=ident[:, :], compare_op=ALU.not_equal, fill=1.0,
                             base=0, pattern=[[-1, P]], channel_multiplier=1).then_inc(s_ident, 1)
            pool.wait_ge(s_consts, 2)

            def iteration(i):
                b, n = shifted(i, 1), shifted(i, 3)
                for g in range(H):
                    if g == 0 and there(b):
                        wait_count(pool, s_var2, b, 1, 1)
                        wait_count(pool, s_y2, b, 1, 0)
                        gp.tensor_tensor(rstd2[:, :], var2[:, :], minus_half[:, :], ALU.pow).then_inc(s_rstd2, 1)
                    if g == 5 and there(n):
                        wait_count(pool, s_var1, n, 1, 1)
                        wait_count(pool, s_y1, n, 1, 0)
                        gp.tensor_tensor(rstd1[:, :], var1[:, :], minus_half[:, :], ALU.pow).then_inc(s_rstd1, 1)
                    if there(i):
                        p = g % 2
                        wait_count(pool, s_inv, i, H, g + 1)
                        wait_count(pool, s_attn_t, i, H, g - 1)
                        pass_waits(pool, s_passed)
                        for t in range(T):
                            last = gp.tensor_scalar(attn[p][:, t, :], probs[p][:, t, :], inv_sum[:, p, t:t + 1], 0.0,
                                                    ALU.mult, ALU.add)
                        last.then_inc(s_attn, 1)
                    if g == 1 and there(i):
                        wait_count(pool, s_x1, i, 1, 1)
                        wait_count(pool, s_added, i, 1, -1)
                        if at_start(i, 0):
                            pool.wait_ge(s_bias_copied, 1)
                        gp.tensor_tensor(x1_biased[i[1] % 2][:, :, :], x1[i[1] % 2][:, :, :],
                                         out_bias[:, :].unsqueeze(1).to_broadcast([P, T, F]), ALU.add)\
                          .then_inc(s_x1_biased, 1)
                    if g == 6 and there(n):
                        wait_count(pool, s_at_hi, n, 1, 1)
                        gp.tensor_tensor(at[1][:, :, :], adjt_sb[(i[1] + 1) % 2][:, :, :],
                                         at[0][:, :, :].bitcast(F32), ALU.subtract).then_inc(s_at_lo, 1)
            run(pool, iteration)


def kernel(x, adj, L0_gnn_W, L1_gnn_Wq, L1_gnn_bq, L1_gnn_Wk, L1_gnn_bk, L1_gnn_Wv, L1_gnn_bv, L1_gnn_Wo, L1_gnn_bo):
    import numpy as np
    import concourse.bacc as bacc
    from concourse.bass_utils import run_bass_kernel_spmd

    x, adj = np.asarray(x), np.asarray(adj)
    B = x.shape[0]

    def weight(w):
        w = np.asarray(w)
        return np.ascontiguousarray(w.T.reshape(-1, P, w.shape[0]).transpose(1, 0, 2))

    def column(v):
        return np.ascontiguousarray(np.asarray(v).reshape(T, P).T)

    a = adj.reshape(B, P, T, P, T)
    arrays = {
        "x": np.ascontiguousarray(x.reshape(B, P, T, F)),
        "adjq": np.ascontiguousarray(a.transpose(0, 1, 2, 4, 3)).reshape(B, P, T, N),
        "adjt": np.ascontiguousarray(a.transpose(0, 3, 4, 2, 1)).reshape(B, P, T, N),
        "w0": weight(L0_gnn_W),
        "wq": weight(L1_gnn_Wq),
        "wk": weight(L1_gnn_Wk),
        "wv": weight(L1_gnn_Wv),
        "wo": weight(L1_gnn_Wo),
        "bq": column(L1_gnn_bq),
        "bk": column(L1_gnn_bk),
        "bv": column(L1_gnn_bv),
        "bo": np.ascontiguousarray(np.asarray(L1_gnn_bo).reshape(1, F)),
    }
    nc = bacc.Bacc("TRN2", target_bir_lowering=False, num_devices=1)
    ins = [nc.dram_tensor(name, v.shape, mybir.dt.from_np(v.dtype), kind="ExternalInput").ap()
           for name, v in arrays.items()]
    out = nc.dram_tensor("out", (B, P, T, F), F32, kind="ExternalOutput").ap()
    build(nc, *ins, out)
    r = run_bass_kernel_spmd(nc, [arrays], core_ids=[0])
    return r.results[0]["out"].reshape(B, N, F)
```

```python
from contextlib import ExitStack

import concourse.bass as bass
from concourse import mybir

ALU = mybir.AluOpType
ACT = mybir.ActivationFunctionType
F32 = mybir.dt.float32
F32R = mybir.dt.float32r

P = 128
N = 256
F = 256
T = N // P
H = 8
D = F // H
G = P // D
LN_EPS = 1e-5
DEG_EPS = 1e-6
SCALE2 = 2.0 * float(D) ** -0.5
LOWEST = -3.0e38

PARTS = ((0, 0), (0, 1), (1, 0))

K_LO, K_HI, Q_HI, Q_LO = range(4)
STACK = ((K_HI, Q_HI), (K_LO, Q_HI), (K_HI, Q_LO))
STACK_ROWS = D * len(STACK)
STACK_INC = 16 * len(STACK)

AHEAD, BEHIND = 5, 2
FIRST_PAIR = 2



def shifted(i, by):
    return (i[0], i[1] + by)


def wait_count(eng, sem, i, per=1, more=0):
    j, c = i
    fixed = per * c + more
    if isinstance(j, int):
        if fixed > 0:
            eng.wait_ge(sem, fixed)
    else:
        assert 2 * per * FIRST_PAIR + fixed > 0
        eng.wait_ge(sem, j * (2 * per) + fixed)


def wait_dma(eng, sems, i, inc=16):
    j, c = i
    sem, fixed = sems[c % 2], inc * (c // 2 + 1)
    if isinstance(j, int):
        if fixed > 0:
            eng.wait_ge(sem, fixed)
    else:
        assert inc * FIRST_PAIR + fixed > 0
        eng.wait_ge(sem, j * inc + fixed)


def pass_waits(eng, s_passed):
    eng.sem_inc(s_passed, 1)


def batch_of(dram, i):
    return dram[i[0] * 2 + i[1]]


def build(nc, x, adjq, adjt, w0, wq, wk, wv, wo, bq, bk, bv, bo, out):
    B = x.shape[0]
    assert B % 2 == 0 and B >= 8 and N == 2 * P and F == 2 * P

    with ExitStack() as ctx:
        def sb(name, shape, dt=F32):
            return ctx.enter_context(nc.sbuf_tensor(name, shape, dt))

        def ps(name):
            return ctx.enter_context(nc.psum_tensor(name, [P, T, 256], F32))

        def sem(name):
            return ctx.enter_context(nc.semaphore(name))

        def sems(name):
            return [sem(f"{name}_of_parity{p}") for p in range(2)]

        w_raw = sb("w_raw", [P, 12, 256])
        w_hi, w_lo = sb("w_hi", [P, 12, 256], F32R), sb("w_lo", [P, 12, 256], F32R)
        W = (w_hi, w_lo)
        W0, WQ, WK, WV, WO = 0, 4, 6, 8, 10
        bq_sb, bk_sb, bv_sb = (sb(n, [P, T]) for n in ("bq_sb", "bk_sb", "bv_sb"))
        bv_wide = sb("bv_wide", [P, T, P])
        bo_row = sb("bo_row", [1, F])
        ones_row = sb("ones_row", [1, P])
        out_bias = sb("out_bias", [P, F])
        ident = sb("ident", [P, P])
        minus_half = sb("minus_half", [P, T])

        x_sb = [sb(f"x_sb{p}", [P, T, F]) for p in range(2)]
        adjt_sb = [sb(f"adjt_sb{p}", [P, T, N]) for p in range(2)]
        adjq_sb = [sb(f"adjq_sb{p}", [P, T, N]) for p in range(2)]
        mask = [sb(f"mask{p}", [P, T, N]) for p in range(2)]
        stats1, stats2 = sb("stats1", [P, T, 6]), sb("stats2", [P, T, 6])
        mv1, mv2 = sb("mv1", [P, T, 2]), sb("mv2", [P, T, 2])
        var1, var2 = sb("var1", [P, T]), sb("var2", [P, T])
        rstd1, rstd2 = sb("rstd1", [P, T]), sb("rstd2", [P, T])
        y1, y2 = sb("y1", [P, T, F]), sb("y2", [P, T, F])
        h1 = (sb("h1_hi", [P, T, F], F32R), sb("h1_lo", [P, T, F], F32R))
        at = (sb("at_hi", [P, T, N], F32R), sb("at_lo", [P, T, N], F32R))
        h1t = (sb("h1t_hi", [P, T, N], F32R), sb("h1t_lo", [P, T, N], F32R))
        aggt = (sb("aggt_hi", [P, T, N], F32R), sb("aggt_lo", [P, T, N], F32R))
        deg_junk = sb("deg_junk", [P, T, N])
        deg, deg_max, deg_inv = sb("deg", [P, T]), sb("deg_max", [P, T]), sb("deg_inv", [P, T])
        self_part = sb("self_part", [P, T, F])
        l0_sum = sb("l0_sum", [P, T, F])
        x1 = [sb(f"x1_{p}", [P, T, F]) for p in range(2)]
        x1_biased = [sb(f"x1_biased{p}", [P, T, F]) for p in range(2)]
        h2t = (sb("h2t_hi", [P, T, N], F32R), sb("h2t_lo", [P, T, N], F32R))
        kq = sb("kq", [P, 4, T, N], F32R)
        kq_stack = [sb(f"kq_stack{p}", [STACK_ROWS, G, 2, T, N], F32R) for p in range(2)]
        v_sb = [sb(f"v_sb{p}", [P, T, F]) for p in range(2)]
        masked = [sb(f"masked{p}", [P, T, N]) for p in range(2)]
        row_max, neg_max = sb("row_max", [P, 2, T]), sb("neg_max", [P, 2, T])
        row_sum, inv_sum = sb("row_sum", [P, 2, T]), sb("inv_sum", [P, 2, T])
        probs = [sb(f"probs{p}", [P, T, N]) for p in range(2)]
        attn = [sb(f"attn{p}", [P, T, N]) for p in range(2)]
        attn_t = sb("attn_t", [P, H, T, N])
        ctxt = (sb("ctxt_hi", [P, T, N], F32R), sb("ctxt_lo", [P, T, N], F32R))
        out_sb = [sb(f"out_sb{p}", [P, T, F]) for p in range(2)]

        ps_s = [ps("ps_s0"), ps("ps_s1")]
        ps_t = [ps("ps_t0"), ps("ps_t1")]
        ps_ctx = ps("ps_ctx")
        ps_front = [ps(f"ps_front{r}") for r in range(3)]

        s_weights = sem("s_weights")
        s_x, s_adjt, s_adjq, s_mask = sems("s_x"), sems("s_adjt"), sems("s_adjq"), sems("s_mask")
        s_stored = sems("s_stored")
        s_stack = [sems(f"s_stack_head{g}") for g in range(G)]
        s_passed = sem("s_passed")
        s_ident = sem("s_ident")
        s_consts = sem("s_consts")
        s_w_hi, s_w_lo = sem("s_w_hi"), sem("s_w_lo")
        s_bv_wide, s_bias_ready, s_bias_copied = sem("s_bv_wide"), sem("s_bias_ready"), sem("s_bias_copied")
        s_scores = sem("s_scores")
        s_masked = sem("s_masked")
        s_negmax = sem("s_negmax")
        s_exp = sem("s_exp")
        s_inv = sem("s_inv")
        s_attn = sem("s_attn")
        s_attn_t = sem("s_attn_t")
        s_attn_copied = sem("s_attn_copied")
        s_ctx_half, s_ctx = sem("s_ctx_half"), sem("s_ctx")
        s_ctx_hi, s_ctx_lo = sem("s_ctx_hi"), sem("s_ctx_lo")
        s_out, s_added = sem("s_out"), sem("s_added")
        s_stats1, s_mv1, s_var1 = sem("s_stats1"), sem("s_mv1"), sem("s_var1")
        s_rstd1, s_y1 = sem("s_rstd1"), sem("s_y1")
        s_h1_hi, s_h1_lo = sem("s_h1_hi"), sem("s_h1_lo")
        s_at_hi, s_at_lo = sem("s_at_hi"), sem("s_at_lo")
        s_y1t, s_h1t_hi, s_h1t_lo = sem("s_y1t"), sem("s_h1t_hi"), sem("s_h1t_lo")
        s_agg, s_agg_hi, s_agg_lo = sem("s_agg"), sem("s_agg_hi"), sem("s_agg_lo")
        s_self, s_self_copied = sem("s_self"), sem("s_self_copied")
        s_nbr = sem("s_nbr")
        s_deg, s_deg_max, s_deg_inv = sem("s_deg"), sem("s_deg_max"), sem("s_deg_inv")
        s_l0_sum, s_x1 = sem("s_l0_sum"), sem("s_x1")
        s_stats2, s_mv2, s_var2 = sem("s_stats2"), sem("s_mv2"), sem("s_var2")
        s_rstd2, s_y2 = sem("s_rstd2"), sem("s_y2")
        s_x1_biased = sem("s_x1_biased")
        s_y2t, s_h2t_hi, s_h2t_lo = sem("s_y2t"), sem("s_h2t_hi"), sem("s_h2t_lo")
        s_q, s_q_hi, s_q_lo = sem("s_q"), sem("s_q_hi"), sem("s_q_lo")
        s_k, s_k_hi, s_k_lo = sem("s_k"), sem("s_k_hi"), sem("s_k_lo")
        s_v, s_v_copied = sem("s_v"), sem("s_v_copied")

        block = ctx.enter_context(nc.Block())

        def there(i, by=0):
            return not isinstance(i[0], int) or 0 <= i[1] + by < B

        def at_start(i, c):
            return isinstance(i[0], int) and i[1] == c

        def head_there(i, g):
            return there(i, g // H)

        def run(eng, iteration):
            last_pair = (B - 2 - AHEAD) // 2
            for c in range(-AHEAD, 2 * FIRST_PAIR):
                iteration((0, c))
            with eng.Fori(FIRST_PAIR, last_pair + 1) as j:
                iteration((j, 0))
                iteration((j, 1))
            for c in range(2 * last_pair + 2, B + BEHIND):
                iteration((0, c))

        @block.sync
        def _(sp):
            weights = ((w_raw[:, W0:W0 + 4, :], w0), (w_raw[:, WQ:WQ + 2, :], wq), (w_raw[:, WK:WK + 2, :], wk),
                       (w_raw[:, WV:WV + 2, :], wv), (w_raw[:, WO:WO + 2, :], wo),
                       (bq_sb[:, :], bq), (bk_sb[:, :], bk), (bv_sb[:, :], bv), (bo_row[:, :], bo))
            def stack(m, g):
                for r, (k_part, q_part) in enumerate(STACK):
                    sp.dma_start(kq_stack[m[1] % 2][D * r:D * r + D, g, :, :, :].bitcast(F32),
                                 kq[D * g:D * g + D, k_part:q_part + 1:q_part - k_part, :, :].bitcast(F32))\
                      .then_inc(s_stack[g][m[1] % 2], 16)

            def iteration(i):
                if there(i, 4):
                    m = shifted(i, 4)
                    wait_count(sp, s_x1, m, 1, -1)
                    pass_waits(sp, s_passed)
                    sp.dma_start(x_sb[m[1] % 2][:, :, :], batch_of(x, m)).then_inc(s_x[m[1] % 2], 16)
                if there(i, -2):
                    m = shifted(i, -2)
                    wait_count(sp, s_added, m, 1, 1)
                    pass_waits(sp, s_passed)
                    sp.dma_start(batch_of(out, m), out_sb[m[1] % 2][:, :, :]).then_inc(s_stored[m[1] % 2], 16)
                if there(i, 1):
                    m = shifted(i, 1)
                    wait_dma(sp, s_adjq, m)
                    pass_waits(sp, s_passed)
                    wait_count(sp, s_masked, m, H, -H)
                    pass_waits(sp, s_passed)
                    sp.dma_start(mask[m[1] % 2][:, :, :], adjq_sb[m[1] % 2][:, :, :]).then_inc(s_mask[m[1] % 2], 16)
                if there(i, 5):
                    m = shifted(i, 5)
                    wait_count(sp, s_at_lo, m, 1, -1)
                    pass_waits(sp, s_passed)
                    sp.dma_start(adjt_sb[m[1] % 2][:, :, :], batch_of(adjt, m)).then_inc(s_adjt[m[1] % 2], 16)
                if there(i, 1):
                    m = shifted(i, 1)
                    stack(m, 1)
                if there(i, 3):
                    m = shifted(i, 3)
                    wait_dma(sp, s_mask, shifted(m, -2))
                    pass_waits(sp, s_passed)
                    wait_count(sp, s_deg, m, 1, -1)
                    pass_waits(sp, s_passed)
                    sp.dma_start(adjq_sb[m[1] % 2][:, :, :], batch_of(adjq, m)).then_inc(s_adjq[m[1] % 2], 16)
                if there(i, 1):
                    m = shifted(i, 1)
                    stack(m, 2)
                if there(i, 1):
                    m = shifted(i, 1)
                    stack(m, 3)
                if there(i, 2):
                    m = shifted(i, 2)
                    wait_count(sp, s_scores, m, H, -H)
                    pass_waits(sp, s_passed)
                    for s_part in (s_q_hi, s_q_lo, s_k_hi, s_k_lo):
                        wait_count(sp, s_part, m, 1, 1)
                        pass_waits(sp, s_passed)
                    stack(m, 0)
                if at_start(i, -AHEAD):
                    for dst, src in weights:
                        sp.dma_start(dst, src).then_inc(s_weights, 16)
            run(sp, iteration)
            for p in range(2):
                sp.wait_ge(s_stored[p], 16 * (B // 2))

        @block.tensor
        def _(pe):
            mm = nc.tensor.matmul

            def product(dst, stationary, moving, first_s=0, first_m=0, tiles=range(T)):
                for o in tiles:
                    for c in range(T):
                        for n, (a, b) in enumerate(PARTS):
                            last = mm(dst[:, o, :], stationary[a][:, first_s + c, o * P:o * P + P],
                                      moving[b][:, first_m + c, :],
                                      start=(c == 0 and n == 0), stop=(c == T - 1 and n == len(PARTS) - 1))
                return last

            def transposed(dst, src):
                for f in range(T):
                    for t in range(T):
                        last = nc.tensor.transpose(dst[:, f, t * P:t * P + P], src[:, t, f * P:f * P + P], ident[:, :])
                return last

            def bank_read(eng, *readers):
                for s_reader, m in readers:
                    if there(m):
                        wait_count(eng, s_reader, m, 1, 1)
                        return

            def scores(i, g):
                p, ft, j = (i[1] + g // H) % 2, g % H // G, g % G
                wait_count(pe, s_masked, i, H, g - 1)
                if ft == 0:
                    wait_dma(pe, s_stack[j], shifted(i, g // H), STACK_INC)
                for t in range(T):
                    last = mm(ps_s[g % 2][:, t, :], kq_stack[p][:, j, 1, ft, t * P:t * P + P], kq_stack[p][:, j, 0, ft, :],
                              start=True, stop=True)
                last.then_inc(s_scores, 1)

            def attn_transposed(i, g):
                wait_count(pe, s_attn, i, H, g + 1)
                wait_count(pe, s_attn_copied, i, H, g - 1)
                transposed(ps_t[g % 2], attn[g % 2]).then_inc(s_attn_t, 1)

            def context(i, ft):
                for c in range(T):
                    for j in range(G):
                        h = G * ft + j
                        last = mm(ps_ctx[D * j:D * j + D, ft, :], v_sb[i[1] % 2][:, c, D * h:D * h + D],
                                  attn_t[:, h, c, :], start=(c == 0), stop=(c == T - 1))
                return last

            pe.wait_ge(s_ident, 2)
            pe.wait_ge(s_consts, 2)
            pe.wait_ge(s_weights, 16 * 9)
            pe.wait_ge(s_bv_wide, 1)
            for c in range(T):
                mm(ps_ctx[:, 0, :], bv_wide[:, c, :], w_raw[:, WO + c, :], start=(c == 0), stop=False)
            mm(ps_ctx[:, 0, :], ones_row[:, :], bo_row[:, :], start=False, stop=True).then_inc(s_bias_ready, 1)
            pe.wait_ge(s_w_hi, 1)
            pe.wait_ge(s_w_lo, 1)

            def iteration(i):
                for g in range(H):
                    if head_there(i, g + 1):
                        scores(i, g + 1)
                    if g == 0 and there(i, -2):
                        m = shifted(i, -2)
                        wait_count(pe, s_ctx_lo, m, 1, 1)
                        bank_read(pe, (s_agg_lo, shifted(m, 4)), (s_q_lo, shifted(m, 2)), (s_added, shifted(m, -1)))
                        product(ps_front[0], ctxt, W, first_m=WO).then_inc(s_out, 1)
                    if g == 1 and there(i, 1):
                        m = shifted(i, 1)
                        wait_count(pe, s_h2t_lo, m, 1, 1)
                        bank_read(pe, (s_self_copied, shifted(m, 1)), (s_v_copied, shifted(m, -1)), (s_k_lo, shifted(m, -1)))
                        product(ps_front[2], W, h2t, first_s=WK).then_inc(s_k, 1)
                    if g == 3 and there(i, -1):
                        m = shifted(i, -1)
                        wait_count(pe, s_attn_copied, m, H, G)
                        wait_count(pe, s_v_copied, m, 1, 1)
                        wait_count(pe, s_ctx_lo, m, 1, 0)
                        if at_start(m, 0):
                            pe.wait_ge(s_bias_copied, 1)
                        context(m, 0).then_inc(s_ctx_half, 1)
                    if head_there(i, g - 3):
                        attn_transposed(i, g - 3)
                    if g == 0 and there(i, 2):
                        m = shifted(i, 2)
                        wait_count(pe, s_agg_lo, m, 1, 1)
                        bank_read(pe, (s_h2t_lo, shifted(m, -1)), (s_h1t_lo, m), (s_l0_sum, shifted(m, -1)))
                        product(ps_front[1], aggt, W, first_m=W0 + T).then_inc(s_nbr, 1)
                    if g == 1 and there(i, 1):
                        m = shifted(i, 1)
                        wait_count(pe, s_h2t_lo, m, 1, 1)
                        bank_read(pe, (s_added, shifted(m, -3)), (s_agg_lo, shifted(m, 1)), (s_q_lo, shifted(m, -1)))
                        product(ps_front[0], W, h2t, first_s=WQ).then_inc(s_q, 1)
                    if g == 2 and there(i, 3):
                        m = shifted(i, 3)
                        wait_count(pe, s_y1, m, 1, 1)
                        bank_read(pe, (s_l0_sum, shifted(m, -1)), (s_h2t_lo, shifted(m, -2)), (s_h1t_lo, shifted(m, -1)))
                        transposed(ps_front[1], y1).then_inc(s_y1t, 1)
                    if g == 3 and there(i, 1):
                        m = shifted(i, 1)
                        wait_count(pe, s_h2t_lo, m, 1, 1)
                        bank_read(pe, (s_k_lo, m), (s_self_copied, shifted(m, 1)), (s_v_copied, shifted(m, -1)))
                        product(ps_front[2], h2t, W, first_m=WV).then_inc(s_v, 1)
                    if g == 3 and there(i, -1):
                        m = shifted(i, -1)
                        wait_count(pe, s_attn_copied, m, H, H)
                        context(m, 1).then_inc(s_ctx, 1)
                    if g == 5 and there(i, 3):
                        m = shifted(i, 3)
                        wait_count(pe, s_h1_hi, m, 1, 1)
                        wait_count(pe, s_h1_lo, m, 1, 1)
                        wait_count(pe, s_at_hi, m, 1, 1)
                        wait_count(pe, s_at_lo, m, 1, 1)
                        bank_read(pe, (s_q_lo, shifted(m, -2)), (s_added, shifted(m, -5)), (s_agg_lo, shifted(m, -1)))
                        product(ps_front[0], h1, at).then_inc(s_agg, 1)
                    if g == 6 and there(i, 2):
                        m = shifted(i, 2)
                        wait_count(pe, s_y2, m, 1, 1)
                        bank_read(pe, (s_h1t_lo, shifted(m, 1)), (s_l0_sum, m), (s_h2t_lo, shifted(m, -1)))
                        transposed(ps_front[1], y2).then_inc(s_y2t, 1)
                    if g == 6 and there(i, 3):
                        m = shifted(i, 3)
                        wait_count(pe, s_h1t_lo, m, 1, 1)
                        bank_read(pe, (s_v_copied, shifted(m, -2)), (s_k_lo, shifted(m, -2)), (s_self_copied, shifted(m, -1)))
                        product(ps_front[2], h1t, W, first_m=W0).then_inc(s_self, 1)
            run(pe, iteration)

        @block.scalar
        def _(act):
            copy = ACT.Copy

            act.wait_ge(s_bias_ready, 1)
            nc.scalar.activation(out_bias[:, :], ps_ctx[:, 0, :], copy).then_inc(s_bias_copied, 1)

            def exponentials(i, g):
                p = g % 2
                wait_count(act, s_negmax, i, H, g + 1)
                wait_count(act, s_attn, i, H, g - 1)
                for t in range(T):
                    last = nc.scalar.activation(probs[p][:, t, :], masked[p][:, t, :], ACT.Exp,
                                                bias=neg_max[:, p, t:t + 1], scale=SCALE2,
                                                accum_out=row_sum[:, p, t:t + 1])
                last.then_inc(s_exp, 1)

            def attn_copy(i, g):
                wait_count(act, s_attn_t, i, H, g + 1)
                used = shifted(i, g // H)
                wait_count(act, s_ctx if g % H >= G else s_ctx_half, used, 1, 0)
                nc.scalar.activation(attn_t[:, g % H, :, :], ps_t[g % 2][:, :, :], copy).then_inc(s_attn_copied, 1)

            def iteration(i):
                for g in range(H):
                    if g == 0 and there(i, 2):
                        m = shifted(i, 2)
                        wait_count(act, s_self, m, 1, 1)
                        wait_count(act, s_l0_sum, m, 1, 0)
                        nc.scalar.activation(self_part[:, :, :], ps_front[2][:, :, :], copy).then_inc(s_self_copied, 1)
                    if g == 3 and there(i, 1):
                        m = shifted(i, 1)
                        wait_count(act, s_k, m, 1, 1)
                        for head in range(G):
                            wait_dma(act, s_stack[head], shifted(m, -1), STACK_INC)
                        for f in range(T):
                            last = nc.scalar.activation(kq[:, K_HI, f, :], ps_front[2][:, f, :], ACT.Identity, bias=bk_sb[:, f:f + 1])
                        last.then_inc(s_k_hi, 1)
                    if g == 3 and there(i, 1):
                        m = shifted(i, 1)
                        wait_count(act, s_q, m, 1, 1)
                        for f in range(T):
                            last = nc.scalar.activation(kq[:, Q_HI, f, :], ps_front[0][:, f, :], ACT.Identity, bias=bq_sb[:, f:f + 1])
                        last.then_inc(s_q_hi, 1)
                    if g == 4 and there(i, 3):
                        m = shifted(i, 3)
                        wait_count(act, s_y1t, m, 1, 1)
                        wait_count(act, s_self, m, 1, 0)
                        nc.scalar.activation(h1t[0][:, :, :], ps_front[1][:, :, :], ACT.Relu).then_inc(s_h1t_hi, 1)
                    if g == 6 and there(i, -1):
                        m = shifted(i, -1)
                        wait_count(act, s_ctx, m, 1, 1)
                        wait_count(act, s_out, m, 1, 0)
                        nc.scalar.activation(ctxt[0][:, :, :], ps_ctx[:, :, :], copy).then_inc(s_ctx_hi, 1)
                    if g == 6 and there(i, 1):
                        m = shifted(i, 1)
                        wait_count(act, s_v, m, 1, 1)
                        wait_count(act, s_ctx, m, 1, -1)
                        nc.scalar.activation(v_sb[m[1] % 2][:, :, :], ps_front[2][:, :, :], copy).then_inc(s_v_copied, 1)
                    if g == 7 and there(i, 3):
                        m = shifted(i, 3)
                        wait_count(act, s_agg, m, 1, 1)
                        wait_count(act, s_nbr, m, 1, 0)
                        nc.scalar.activation(aggt[0][:, :, :], ps_front[0][:, :, :], copy).then_inc(s_agg_hi, 1)
                    if g == 7 and there(i, 2):
                        m = shifted(i, 2)
                        wait_count(act, s_y2t, m, 1, 1)
                        wait_count(act, s_v, m, 1, 0)
                        nc.scalar.activation(h2t[0][:, :, :], ps_front[1][:, :, :], ACT.Relu).then_inc(s_h2t_hi, 1)
                    if head_there(i, g - 1):
                        exponentials(i, g - 1)
                    if g == 0 and there(i, 2):
                        m = shifted(i, 2)
                        wait_dma(act, s_adjq, m)
                        wait_count(act, s_deg_max, m, 1, 0)
                        for t in range(T):
                            last = nc.scalar.activation(deg_junk[:, t, :], adjq_sb[m[1] % 2][:, t, :], copy,
                                                        accum_out=deg[:, t:t + 1])
                        last.then_inc(s_deg, 1)
                    if g == 1 and there(i, 3):
                        m = shifted(i, 3)
                        wait_count(act, s_y1, m, 1, 1)
                        wait_count(act, s_agg, m, 1, 0)
                        nc.scalar.activation(h1[0][:, :, :], y1[:, :, :], ACT.Relu).then_inc(s_h1_hi, 1)
                    if head_there(i, g - 4):
                        attn_copy(i, g - 4)
            run(act, iteration)

        @block.vector
        def _(dve):
            v = nc.vector
            f32 = lambda ap: ap.bitcast(F32)

            def split_weights():
                dve.wait_ge(s_weights, 16 * 9)
                v.tensor_copy(bv_wide[:, :, :], bv_sb[:, :].unsqueeze(2).to_broadcast([P, T, P])).then_inc(s_bv_wide, 1)
                v.tensor_copy(w_hi[:, :, :], w_raw[:, :, :]).then_inc(s_w_hi, 1)
                dve.wait_ge(s_w_hi, 1)
                v.tensor_tensor(w_lo[:, :, :], w_raw[:, :, :], f32(w_hi[:, :, :]), ALU.subtract).then_inc(s_w_lo, 1)

            def statistics(m, src, stats, mv, s_stats, s_mv):
                for t in range(T):
                    last = v.bn_stats(stats[:, t, :], src[:, t, :])
                last.then_inc(s_stats, 1)
                wait_count(dve, s_stats, m, 1, 1)
                pass_waits(dve, s_passed)
                for t in range(T):
                    last = v.bn_aggr(mv[:, t, :], stats[:, t, :])
                last.then_inc(s_mv, 1)

            def normalised(dst, src, mv, rstd):
                for t in range(T):
                    last = v.tensor_scalar(dst[:, t, :], src[:, t, :], mv[:, t, 0:1], rstd[:, t:t + 1],
                                           ALU.subtract, ALU.mult)
                return last

            def masked_scores(i, g):
                p, m = g % 2, (i[1] + g // H) % 2
                wait_count(dve, s_scores, i, H, g + 1)
                wait_count(dve, s_exp, i, H, g - 1)
                if g % H == 0:
                    wait_dma(dve, s_mask, shifted(i, g // H))
                pass_waits(dve, s_passed)
                for t in range(T):
                    last = v.tensor_tensor_reduce(out=masked[p][:, t, :], in0=ps_s[p][:, t, :], in1=mask[m][:, t, :],
                                                  scale=1.0, scalar=LOWEST, op0=ALU.mult, op1=ALU.max,
                                                  accum_out=row_max[:, p, t:t + 1])
                last.then_inc(s_masked, 1)

            def inverse_sums(i, g):
                p = g % 2
                wait_count(dve, s_exp, i, H, g + 1)
                wait_count(dve, s_attn, i, H, g - 1)
                v.reciprocal(inv_sum[:, p, :], row_sum[:, p, :]).then_inc(s_inv, 1)

            def iteration(i):
                if at_start(i, -AHEAD):
                    split_weights()
                for g in range(H):
                    if head_there(i, g + 1):
                        masked_scores(i, g + 1)
                    if g == 0 and there(i, 2):
                        m = shifted(i, 2)
                        wait_count(dve, s_deg, m, 1, 1)
                        v.tensor_scalar(deg_max[:, :], deg[:, :], DEG_EPS, None, ALU.max).then_inc(s_deg_max, 1)
                        wait_count(dve, s_deg_max, m, 1, 1)
                        wait_count(dve, s_l0_sum, m, 1, 0)
                        v.reciprocal(deg_inv[:, :], deg_max[:, :]).then_inc(s_deg_inv, 1)
                    if g == 0 and there(i, 2):
                        m = shifted(i, 2)
                        wait_count(dve, s_deg_inv, m, 1, 1)
                        wait_count(dve, s_nbr, m, 1, 1)
                        wait_count(dve, s_self_copied, m, 1, 1)
                        for t in range(T):
                            last = v.scalar_tensor_tensor(l0_sum[:, t, :], ps_front[1][:, t, :], deg_inv[:, t:t + 1],
                                                          self_part[:, t, :], ALU.mult, ALU.add)
                        last.then_inc(s_l0_sum, 1)
                    if g == 1 and there(i, 2):
                        m = shifted(i, 2)
                        wait_count(dve, s_l0_sum, m, 1, 1)
                        wait_count(dve, s_x1_biased, m, 1, -1)
                        v.scalar_tensor_tensor(x1[m[1] % 2][:, :, :], l0_sum[:, :, :], 0.0, x_sb[m[1] % 2][:, :, :],
                                               ALU.max, ALU.add).then_inc(s_x1, 1)
                    if g == 1 and there(i, 2):
                        m = shifted(i, 2)
                        wait_count(dve, s_x1, m, 1, 1)
                        wait_count(dve, s_rstd2, m, 1, 0)
                        wait_count(dve, s_y2, m, 1, 0)
                        statistics(m, x1[m[1] % 2], stats2, mv2, s_stats2, s_mv2)
                    if g == 2 and there(i, 1):
                        m = shifted(i, 1)
                        wait_count(dve, s_k_hi, m, 1, 1)
                        for f in range(T):
                            last = v.scalar_tensor_tensor(kq[:, K_LO, f, :], ps_front[2][:, f, :], bk_sb[:, f:f + 1],
                                                          f32(kq[:, K_HI, f, :]), ALU.add, ALU.subtract)
                        last.then_inc(s_k_lo, 1)
                    if g == 2 and there(i, 1):
                        m = shifted(i, 1)
                        wait_count(dve, s_q_hi, m, 1, 1)
                        for f in range(T):
                            last = v.scalar_tensor_tensor(kq[:, Q_LO, f, :], ps_front[0][:, f, :], bq_sb[:, f:f + 1],
                                                          f32(kq[:, Q_HI, f, :]), ALU.add, ALU.subtract)
                        last.then_inc(s_q_lo, 1)
                    if g == 3 and there(i, 3):
                        m = shifted(i, 3)
                        wait_count(dve, s_h1_hi, m, 1, 1)
                        v.scalar_tensor_tensor(h1[1][:, :, :], y1[:, :, :], 0.0, f32(h1[0][:, :, :]),
                                               ALU.max, ALU.subtract).then_inc(s_h1_lo, 1)
                    if g == 3 and there(i, 3):
                        m = shifted(i, 3)
                        wait_count(dve, s_h1t_hi, m, 1, 1)
                        v.scalar_tensor_tensor(h1t[1][:, :, :], ps_front[1][:, :, :], 0.0, f32(h1t[0][:, :, :]),
                                               ALU.max, ALU.subtract).then_inc(s_h1t_lo, 1)
                    if g == 4 and there(i, 2):
                        m = shifted(i, 2)
                        wait_count(dve, s_rstd2, m, 1, 1)
                        wait_count(dve, s_y2t, m, 1, 0)
                        normalised(y2, x1[m[1] % 2], mv2, rstd2).then_inc(s_y2, 1)
                    if g == 5 and there(i, -1):
                        m = shifted(i, -1)
                        wait_count(dve, s_ctx_hi, m, 1, 1)
                        v.tensor_tensor(ctxt[1][:, :, :], ps_ctx[:, :, :], f32(ctxt[0][:, :, :]), ALU.subtract)\
                         .then_inc(s_ctx_lo, 1)
                    if g == 5 and there(i, 4):
                        m = shifted(i, 4)
                        wait_dma(dve, s_x, m)
                        wait_count(dve, s_rstd1, m, 1, 0)
                        wait_count(dve, s_y1, m, 1, 0)
                        statistics(m, x_sb[m[1] % 2], stats1, mv1, s_stats1, s_mv1)
                    if g == 6 and there(i, 3):
                        m = shifted(i, 3)
                        wait_count(dve, s_agg_hi, m, 1, 1)
                        v.tensor_tensor(aggt[1][:, :, :], ps_front[0][:, :, :], f32(aggt[0][:, :, :]), ALU.subtract)\
                         .then_inc(s_agg_lo, 1)
                    if g == 6 and there(i, 2):
                        m = shifted(i, 2)
                        wait_count(dve, s_h2t_hi, m, 1, 1)
                        v.scalar_tensor_tensor(h2t[1][:, :, :], ps_front[1][:, :, :], 0.0, f32(h2t[0][:, :, :]),
                                               ALU.max, ALU.subtract).then_inc(s_h2t_lo, 1)
                    if g == 6 and there(i, 4):
                        m = shifted(i, 4)
                        wait_dma(dve, s_adjt, m)
                        wait_count(dve, s_agg, m, 1, 0)
                        v.tensor_copy(at[0][:, :, :], adjt_sb[m[1] % 2][:, :, :]).then_inc(s_at_hi, 1)
                    if g == 7 and there(i, 4):
                        m = shifted(i, 4)
                        wait_count(dve, s_rstd1, m, 1, 1)
                        wait_count(dve, s_y1t, m, 1, 0)
                        wait_count(dve, s_h1_lo, m, 1, 0)
                        normalised(y1, x_sb[m[1] % 2], mv1, rstd1).then_inc(s_y1, 1)
                    if g == 7 and there(i, -1):
                        m = shifted(i, -1)
                        wait_count(dve, s_out, m, 1, 1)
                        wait_count(dve, s_x1_biased, m, 1, 1)
                        wait_dma(dve, s_stored, shifted(m, -2))
                        v.tensor_tensor(out_sb[m[1] % 2][:, :, :], ps_front[0][:, :, :], x1_biased[m[1] % 2][:, :, :], ALU.add)\
                         .then_inc(s_added, 1)
                    if head_there(i, g):
                        inverse_sums(i, g)
            run(dve, iteration)

        @block.gpsimd
        def _(pool):
            gp = nc.gpsimd
            gp.memset(ident[:, :], 0.0).then_inc(s_ident, 1)
            gp.memset(ones_row[:, :], 1.0).then_inc(s_consts, 1)
            gp.memset(minus_half[:, :], -0.5).then_inc(s_consts, 1)
            pool.wait_ge(s_ident, 1)
            gp.affine_select(out=ident[:, :], in_=ident[:, :], compare_op=ALU.not_equal, fill=1.0,
                             base=0, pattern=[[-1, P]], channel_multiplier=1).then_inc(s_ident, 1)
            pool.wait_ge(s_consts, 2)

            def negative_maxima(i, g):
                p = g % 2
                wait_count(pool, s_masked, i, H, g + 1)
                pass_waits(pool, s_passed)
                gp.tensor_scalar(neg_max[:, p, :], row_max[:, p, :], -SCALE2, 0.0, ALU.mult, ALU.add)\
                  .then_inc(s_negmax, 1)

            def normalised_heads(i, g):
                p = g % 2
                wait_count(pool, s_inv, i, H, g + 1)
                wait_count(pool, s_attn_t, i, H, g - 1)
                pass_waits(pool, s_passed)
                for t in range(T):
                    last = gp.tensor_scalar(attn[p][:, t, :], probs[p][:, t, :], inv_sum[:, p, t:t + 1], 0.0,
                                            ALU.mult, ALU.add)
                last.then_inc(s_attn, 1)

            def iteration(i):
                for g in range(H):
                    if g == 1 and there(i):
                        m = i
                        wait_count(pool, s_x1, m, 1, 1)
                        wait_count(pool, s_added, m, 1, -1)
                        if at_start(m, 0):
                            pool.wait_ge(s_bias_copied, 1)
                        gp.tensor_tensor(x1_biased[m[1] % 2][:, :, :], x1[m[1] % 2][:, :, :],
                                         out_bias[:, :].unsqueeze(1).to_broadcast([P, T, F]), ALU.add).then_inc(s_x1_biased, 1)
                    if g == 2 and there(i, 3):
                        m = shifted(i, 3)
                        wait_count(pool, s_at_hi, m, 1, 1)
                        gp.tensor_tensor(at[1][:, :, :], adjt_sb[m[1] % 2][:, :, :], at[0][:, :, :].bitcast(F32),
                                         ALU.subtract).then_inc(s_at_lo, 1)
                    if g == 3 and there(i, 2):
                        m = shifted(i, 2)
                        wait_count(pool, s_mv2, m, 1, 1)
                        wait_count(pool, s_y2, m, 1, 0)
                        pass_waits(pool, s_passed)
                        gp.tensor_scalar(var2[:, :], mv2[:, :, 1], LN_EPS, 0.0, ALU.add, ALU.add).then_inc(s_var2, 1)
                        wait_count(pool, s_var2, m, 1, 1)
                        gp.tensor_tensor(rstd2[:, :], var2[:, :], minus_half[:, :], ALU.pow).then_inc(s_rstd2, 1)
                    if g == 6 and there(i, 4):
                        m = shifted(i, 4)
                        wait_count(pool, s_mv1, m, 1, 1)
                        wait_count(pool, s_y1, m, 1, 0)
                        pass_waits(pool, s_passed)
                        gp.tensor_scalar(var1[:, :], mv1[:, :, 1], LN_EPS, 0.0, ALU.add, ALU.add).then_inc(s_var1, 1)
                        wait_count(pool, s_var1, m, 1, 1)
                        gp.tensor_tensor(rstd1[:, :], var1[:, :], minus_half[:, :], ALU.pow).then_inc(s_rstd1, 1)
                    if head_there(i, g - 1):
                        normalised_heads(i, g - 1)
                    if head_there(i, g + 1):
                        negative_maxima(i, g + 1)
            run(pool, iteration)


def kernel(x, adj, L0_gnn_W, L1_gnn_Wq, L1_gnn_bq, L1_gnn_Wk, L1_gnn_bk, L1_gnn_Wv, L1_gnn_bv, L1_gnn_Wo, L1_gnn_bo):
    import numpy as np
    import concourse.bacc as bacc
    from concourse.bass_utils import run_bass_kernel_spmd

    x, adj = np.asarray(x), np.asarray(adj)
    B = x.shape[0]

    def weight(w):
        w = np.asarray(w)
        return np.ascontiguousarray(w.T.reshape(-1, P, w.shape[0]).transpose(1, 0, 2))

    def column(v):
        return np.ascontiguousarray(np.asarray(v).reshape(T, P).T)

    a = adj.reshape(B, P, T, P, T)
    arrays = {
        "x": np.ascontiguousarray(x.reshape(B, P, T, F)),
        "adjq": np.ascontiguousarray(a.transpose(0, 1, 2, 4, 3)).reshape(B, P, T, N),
        "adjt": np.ascontiguousarray(a.transpose(0, 3, 4, 2, 1)).reshape(B, P, T, N),
        "w0": weight(L0_gnn_W),
        "wq": weight(L1_gnn_Wq),
        "wk": weight(L1_gnn_Wk),
        "wv": weight(L1_gnn_Wv),
        "wo": weight(L1_gnn_Wo),
        "bq": column(L1_gnn_bq),
        "bk": column(L1_gnn_bk),
        "bv": column(L1_gnn_bv),
        "bo": np.ascontiguousarray(np.asarray(L1_gnn_bo).reshape(1, F)),
    }
    nc = bacc.Bacc("TRN2", target_bir_lowering=False, num_devices=1)
    ins = [nc.dram_tensor(name, v.shape, mybir.dt.from_np(v.dtype), kind="ExternalInput").ap()
           for name, v in arrays.items()]
    out = nc.dram_tensor("out", (B, P, T, F), F32, kind="ExternalOutput").ap()
    build(nc, *ins, out)
    r = run_bass_kernel_spmd(nc, [arrays], core_ids=[0])
    return r.results[0]["out"].reshape(B, N, F)
```

```python
from contextlib import ExitStack

import concourse.bass as bass
from concourse import mybir

ALU = mybir.AluOpType
ACT = mybir.ActivationFunctionType
F32 = mybir.dt.float32
F32R = mybir.dt.float32r

P = 128
N = 256
F = 256
T = N // P
H = 8
D = F // H
G = P // D
LN_EPS = 1e-5
DEG_EPS = 1e-6
SCALE2 = 2.0 * float(D) ** -0.5
LOWEST = -3.0e38

PARTS = ((0, 0), (0, 1), (1, 0))

K_LO, K_HI, Q_HI, Q_LO = range(4)
STACK = ((K_HI, Q_HI), (K_LO, Q_HI), (K_HI, Q_LO))
STACK_ROWS = D * len(STACK)
STACK_INC = 16 * len(STACK)

AHEAD, BEHIND = 4, 3
FIRST_PAIR = 2



def shifted(i, by):
    return (i[0], i[1] + by)


def wait_count(eng, sem, i, per=1, more=0):
    j, c = i
    fixed = per * c + more
    if isinstance(j, int):
        if fixed > 0:
            eng.wait_ge(sem, fixed)
    else:
        assert 2 * per * FIRST_PAIR + fixed > 0
        eng.wait_ge(sem, j * (2 * per) + fixed)


def wait_dma(eng, sems, i, inc=16):
    j, c = i
    sem, fixed = sems[c % 2], inc * (c // 2 + 1)
    if isinstance(j, int):
        if fixed > 0:
            eng.wait_ge(sem, fixed)
    else:
        assert inc * FIRST_PAIR + fixed > 0
        eng.wait_ge(sem, j * inc + fixed)


def pass_waits(eng, s_passed):
    eng.sem_inc(s_passed, 1)


def batch_of(dram, i):
    return dram[i[0] * 2 + i[1]]


def build(nc, x, adjq, adjt, w0, wq, wk, wv, wo, bq, bk, bv, bo, out):
    B = x.shape[0]
    assert B % 2 == 0 and B >= 16 and N == 2 * P and F == 2 * P

    with ExitStack() as ctx:
        def sb(name, shape, dt=F32):
            return ctx.enter_context(nc.sbuf_tensor(name, shape, dt))

        def ps(name):
            return ctx.enter_context(nc.psum_tensor(name, [P, T, 256], F32))

        def sem(name):
            return ctx.enter_context(nc.semaphore(name))

        def sems(name):
            return [sem(f"{name}_of_parity{p}") for p in range(2)]

        w_raw = sb("w_raw", [P, 12, 256])
        w_hi, w_lo = sb("w_hi", [P, 12, 256], F32R), sb("w_lo", [P, 12, 256], F32R)
        W = (w_hi, w_lo)
        W0, WQ, WK, WV, WO = 0, 4, 6, 8, 10
        bq_sb, bk_sb, bv_sb = (sb(n, [P, T]) for n in ("bq_sb", "bk_sb", "bv_sb"))
        bv_wide = sb("bv_wide", [P, T, P])
        bo_row = sb("bo_row", [1, F])
        ones_row = sb("ones_row", [1, P])
        out_bias = sb("out_bias", [P, F])
        ident = sb("ident", [P, P])
        minus_half = sb("minus_half", [P, T])

        x_sb = [sb(f"x_sb{p}", [P, T, F]) for p in range(2)]
        adjt_sb = [sb(f"adjt_sb{p}", [P, T, N]) for p in range(2)]
        adjq_sb = [sb(f"adjq_sb{p}", [P, T, N]) for p in range(2)]
        mask = [sb(f"mask{p}", [P, T, N]) for p in range(2)]
        stats1, stats2 = sb("stats1", [P, T, 6]), sb("stats2", [P, T, 6])
        mv1, mv2 = sb("mv1", [P, T, 2]), sb("mv2", [P, T, 2])
        var1, var2 = sb("var1", [P, T]), sb("var2", [P, T])
        rstd1, rstd2 = sb("rstd1", [P, T]), sb("rstd2", [P, T])
        y1, y2 = sb("y1", [P, T, F]), sb("y2", [P, T, F])
        at = (sb("at_hi", [P, T, N], F32R), sb("at_lo", [P, T, N], F32R))
        h1t = (sb("h1t_hi", [P, T, N], F32R), sb("h1t_lo", [P, T, N], F32R))
        nbr_in = (sb("nbr_in_hi", [P, T, F], F32R), sb("nbr_in_lo", [P, T, F], F32R))
        deg, deg_max, deg_inv = sb("deg", [P, T]), sb("deg_max", [P, T]), sb("deg_inv", [P, T])
        self_part = sb("self_part", [P, T, F])
        l0_sum = sb("l0_sum", [P, T, F])
        x1 = [sb(f"x1_{p}", [P, T, F]) for p in range(2)]
        x1_biased = [sb(f"x1_biased{p}", [P, T, F]) for p in range(2)]
        h2t = (sb("h2t_hi", [P, T, N], F32R), sb("h2t_lo", [P, T, N], F32R))
        kq = [sb(f"kq{p}", [P, 4, T, N], F32R) for p in range(2)]
        kq_stack = [sb(f"kq_stack{p}", [STACK_ROWS, G, 2, T, N], F32R) for p in range(2)]
        v_sb = [sb(f"v_sb{p}", [P, T, F]) for p in range(2)]
        masked = [sb(f"masked{p}", [P, T, N]) for p in range(2)]
        row_max, neg_max = sb("row_max", [P, 2, T]), sb("neg_max", [P, 2, T])
        row_sum, inv_sum = sb("row_sum", [P, 2, T]), sb("inv_sum", [P, 2, T])
        probs = [sb(f"probs{p}", [P, T, N]) for p in range(2)]
        attn = [sb(f"attn{p}", [P, T, N]) for p in range(2)]
        attn_t = sb("attn_t", [P, H, T, N])
        ctxt = (sb("ctxt_hi", [P, T, N], F32R), sb("ctxt_lo", [P, T, N], F32R))
        out_sb = [sb(f"out_sb{p}", [P, T, F]) for p in range(2)]

        ps_s = [ps("ps_s0"), ps("ps_s1")]
        ps_t = [ps("ps_t0"), ps("ps_t1")]
        ps_ctx = ps("ps_ctx")
        ps_front = [ps(f"ps_front{r}") for r in range(3)]

        s_weights_first, s_weights = sem("s_weights_first"), sem("s_weights")
        s_x, s_adjt, s_adjq, s_mask = sems("s_x"), sems("s_adjt"), sems("s_adjq"), sems("s_mask")
        s_stored = sems("s_stored")
        s_stack = [sems(f"s_stack_head{g}") for g in range(G)]
        s_passed = sem("s_passed")
        s_ident = sem("s_ident")
        s_consts = sem("s_consts")
        s_w_hi, s_w_lo = sem("s_w_hi"), sem("s_w_lo")
        s_bv_wide, s_bias_ready, s_bias_copied = sem("s_bv_wide"), sem("s_bias_ready"), sem("s_bias_copied")
        s_scores = sem("s_scores")
        s_masked = sem("s_masked")
        s_negmax = sem("s_negmax")
        s_exp = sem("s_exp")
        s_inv = sem("s_inv")
        s_attn = sem("s_attn")
        s_attn_t = sem("s_attn_t")
        s_attn_copied = sem("s_attn_copied")
        s_ctx_half, s_ctx = sem("s_ctx_half"), sem("s_ctx")
        s_ctx_hi, s_ctx_lo = sem("s_ctx_hi"), sem("s_ctx_lo")
        s_out, s_added = sem("s_out"), sem("s_added")
        s_stats1, s_mv1, s_var1 = sem("s_stats1"), sem("s_mv1"), sem("s_var1")
        s_rstd1, s_y1 = sem("s_rstd1"), sem("s_y1")
        s_at_hi, s_at_lo = sem("s_at_hi"), sem("s_at_lo")
        s_y1t, s_h1t_hi, s_h1t_lo = sem("s_y1t"), sem("s_h1t_hi"), sem("s_h1t_lo")
        s_nbr_in, s_nbr_in_hi, s_nbr_in_lo = sem("s_nbr_in"), sem("s_nbr_in_hi"), sem("s_nbr_in_lo")
        s_self, s_self_copied = sem("s_self"), sem("s_self_copied")
        s_nbr = sem("s_nbr")
        s_deg, s_deg_max, s_deg_inv = sem("s_deg"), sem("s_deg_max"), sem("s_deg_inv")
        s_l0_sum, s_x1 = sem("s_l0_sum"), sem("s_x1")
        s_stats2, s_mv2, s_var2 = sem("s_stats2"), sem("s_mv2"), sem("s_var2")
        s_rstd2, s_y2 = sem("s_rstd2"), sem("s_y2")
        s_x1_biased = sem("s_x1_biased")
        s_y2t, s_h2t_hi, s_h2t_lo = sem("s_y2t"), sem("s_h2t_hi"), sem("s_h2t_lo")
        s_q, s_q_hi, s_q_lo = sem("s_q"), sem("s_q_hi"), sem("s_q_lo")
        s_k, s_k_hi, s_k_lo = sem("s_k"), sem("s_k_hi"), sem("s_k_lo")
        s_v, s_v_copied = sem("s_v"), sem("s_v_copied")

        block = ctx.enter_context(nc.Block())

        def there(i, by=0):
            return not isinstance(i[0], int) or 0 <= i[1] + by < B

        def at_start(i, c):
            return isinstance(i[0], int) and i[1] == c

        def head_there(i, g):
            return there(i, g // H)

        def run(eng, iteration):
            last_pair = (B - 2 - AHEAD) // 2
            for c in range(-AHEAD, 2 * FIRST_PAIR):
                iteration((0, c))
            with eng.Fori(FIRST_PAIR, last_pair + 1) as j:
                iteration((j, 0))
                iteration((j, 1))
            for c in range(2 * last_pair + 2, B + BEHIND):
                iteration((0, c))

        @block.sync
        def _(sp):
            def load_weights():
                for dst, src in ((w_raw[:, W0:WQ, :], w0), (bv_sb[:, :], bv)):
                    sp.dma_start(dst, src).then_inc(s_weights_first, 16)
                for dst, src in ((w_raw[:, WO:WO + T, :], wo), (bo_row[:, :], bo), (w_raw[:, WQ:WQ + T, :], wq),
                                 (w_raw[:, WK:WK + T, :], wk), (w_raw[:, WV:WV + T, :], wv),
                                 (bq_sb[:, :], bq), (bk_sb[:, :], bk)):
                    sp.dma_start(dst, src).then_inc(s_weights, 16)

            def stack(m, g):
                for r, (k_part, q_part) in enumerate(STACK):
                    sp.dma_start(kq_stack[m[1] % 2][D * r:D * r + D, g, :, :, :].bitcast(F32),
                                 kq[m[1] % 2][D * g:D * g + D, k_part:q_part + 1:q_part - k_part, :, :].bitcast(F32))\
                      .then_inc(s_stack[g][m[1] % 2], 16)

            def iteration(i):
                if there(i, 3):
                    m = shifted(i, 3)
                    wait_count(sp, s_x1, m, 1, -1)
                    pass_waits(sp, s_passed)
                    sp.dma_start(x_sb[m[1] % 2][:, :, :], batch_of(x, m)).then_inc(s_x[m[1] % 2], 16)
                if there(i):
                    m = i
                    stack(m, 1)
                if there(i, 2):
                    m = shifted(i, 2)
                    wait_dma(sp, s_mask, shifted(m, -2))
                    pass_waits(sp, s_passed)
                    wait_count(sp, s_deg, m, 1, -1)
                    pass_waits(sp, s_passed)
                    sp.dma_start(adjq_sb[m[1] % 2][:, :, :], batch_of(adjq, m)).then_inc(s_adjq[m[1] % 2], 16)
                if there(i, -3):
                    m = shifted(i, -3)
                    wait_count(sp, s_added, m, 1, 1)
                    pass_waits(sp, s_passed)
                    sp.dma_start(batch_of(out, m), out_sb[m[1] % 2][:, :, :]).then_inc(s_stored[m[1] % 2], 16)
                if there(i, 3):
                    m = shifted(i, 3)
                    wait_count(sp, s_at_lo, m, 1, -1)
                    pass_waits(sp, s_passed)
                    sp.dma_start(adjt_sb[m[1] % 2][:, :, :], batch_of(adjt, m)).then_inc(s_adjt[m[1] % 2], 16)
                    if at_start(m, 0):
                        load_weights()
                if there(i):
                    m = i
                    stack(m, 2)
                if there(i, 1):
                    m = shifted(i, 1)
                    wait_dma(sp, s_adjq, m)
                    pass_waits(sp, s_passed)
                    wait_count(sp, s_masked, m, H, -H)
                    pass_waits(sp, s_passed)
                    sp.dma_start(mask[m[1] % 2][:, :, :], adjq_sb[m[1] % 2][:, :, :]).then_inc(s_mask[m[1] % 2], 16)
                if there(i):
                    m = i
                    stack(m, 3)
                if there(i, 1):
                    m = shifted(i, 1)
                    wait_count(sp, s_scores, m, H, -H)
                    pass_waits(sp, s_passed)
                    for s_part in (s_q_hi, s_q_lo, s_k_hi, s_k_lo):
                        wait_count(sp, s_part, m, 1, 1)
                        pass_waits(sp, s_passed)
                    stack(m, 0)
            run(sp, iteration)
            for p in range(2):
                sp.wait_ge(s_stored[p], 16 * (B // 2))

        @block.tensor
        def _(pe):
            mm = nc.tensor.matmul

            def product(dst, stationary, moving, first_s=0, first_m=0):
                for o in range(T):
                    for c in range(T):
                        for n, (a, b) in enumerate(PARTS):
                            last = mm(dst[:, o, :], stationary[a][:, first_s + c, o * P:o * P + P],
                                      moving[b][:, first_m + c, :],
                                      start=(c == 0 and n == 0), stop=(c == T - 1 and n == len(PARTS) - 1))
                return last

            def transposed(dst, src):
                for f in range(T):
                    for t in range(T):
                        last = nc.tensor.transpose(dst[:, f, t * P:t * P + P], src[:, t, f * P:f * P + P], ident[:, :])
                return last

            def bank_read(eng, *readers):
                for s_reader, m in readers:
                    if there(m):
                        wait_count(eng, s_reader, m, 1, 1)
                        return

            def scores(i, g):
                p, ft, j = (i[1] + g // H) % 2, g % H // G, g % G
                wait_count(pe, s_masked, i, H, g - 1)
                if ft == 0:
                    wait_dma(pe, s_stack[j], shifted(i, g // H), STACK_INC)
                for t in range(T):
                    last = mm(ps_s[g % 2][:, t, :], kq_stack[p][:, j, 1, ft, t * P:t * P + P],
                              kq_stack[p][:, j, 0, ft, :],
                              start=True, stop=True)
                last.then_inc(s_scores, 1)

            def attn_transposed(i, g):
                wait_count(pe, s_attn, i, H, g + 1)
                wait_count(pe, s_attn_copied, i, H, g - 1)
                transposed(ps_t[g % 2], attn[g % 2]).then_inc(s_attn_t, 1)

            def context(i, ft):
                for c in range(T):
                    for j in range(G):
                        h = G * ft + j
                        last = mm(ps_ctx[D * j:D * j + D, ft, :], v_sb[i[1] % 2][:, c, D * h:D * h + D],
                                  attn_t[:, h, c, :], start=(c == 0), stop=(c == T - 1))
                return last

            def output_bias():
                pe.wait_ge(s_consts, 2)
                pe.wait_ge(s_weights, 16 * 7)
                pe.wait_ge(s_bv_wide, 1)
                for c in range(T):
                    mm(ps_ctx[:, 0, :], bv_wide[:, c, :], w_raw[:, WO + c, :], start=(c == 0), stop=False)
                mm(ps_ctx[:, 0, :], ones_row[:, :], bo_row[:, :], start=False, stop=True)\
                  .then_inc(s_bias_ready, 1)

            pe.wait_ge(s_ident, 2)

            def iteration(i):
                for g in range(H):
                    if head_there(i, g + 1):
                        scores(i, g + 1)
                    if g == 0 and there(i, -2):
                        m = shifted(i, -2)
                        wait_count(pe, s_ctx_lo, m, 1, 1)
                        bank_read(pe, (s_self_copied, shifted(m, 4)),
                                      (s_v_copied, shifted(m, 2)),
                                      (s_added, shifted(m, -1)))
                        product(ps_front[0], ctxt, W, first_m=WO).then_inc(s_out, 1)
                    if g == 1 and there(i, 3):
                        m = shifted(i, 3)
                        wait_count(pe, s_y1, m, 1, 1)
                        bank_read(pe, (s_k_lo, shifted(m, -2)),
                                      (s_h2t_lo, shifted(m, -2)),
                                      (s_h1t_lo, shifted(m, -1)))
                        transposed(ps_front[2], y1).then_inc(s_y1t, 1)
                    if g == 4 and there(i, -1):
                        m = shifted(i, -1)
                        wait_count(pe, s_attn_copied, m, H, H)
                        context(m, 1).then_inc(s_ctx, 1)
                    if g == 5 and there(i, 3):
                        m = shifted(i, 3)
                        if at_start(m, 0):
                            pe.wait_ge(s_w_lo, 1)
                        wait_count(pe, s_h1t_lo, m, 1, 1)
                        bank_read(pe, (s_v_copied, shifted(m, -2)),
                                      (s_added, shifted(m, -5)),
                                      (s_self_copied, shifted(m, -1)))
                        product(ps_front[0], h1t, W, first_m=W0).then_inc(s_self, 1)
                    if g == 7 and there(i, 2):
                        m = shifted(i, 2)
                        if at_start(m, 0):
                            pe.wait_ge(s_w_hi, 2)
                            pe.wait_ge(s_w_lo, 2)
                        wait_count(pe, s_h2t_lo, m, 1, 1)
                        bank_read(pe, (s_nbr_in_lo, shifted(m, 1)), (s_l0_sum, m), (s_q_lo, shifted(m, -1)))
                        product(ps_front[1], W, h2t, first_s=WQ).then_inc(s_q, 1)
                        wait_count(pe, s_h2t_lo, m, 1, 1)
                        bank_read(pe, (s_h2t_lo, m), (s_h1t_lo, shifted(m, 1)), (s_k_lo, shifted(m, -1)))
                        product(ps_front[2], W, h2t, first_s=WK).then_inc(s_k, 1)
                    if head_there(i, g - 3):
                        attn_transposed(i, g - 3)
                    if g == 0 and there(i, 2):
                        m = shifted(i, 2)
                        if at_start(m, 0):
                            output_bias()
                        wait_count(pe, s_nbr_in_lo, m, 1, 1)
                        wait_count(pe, s_at_hi, m, 1, 1)
                        wait_count(pe, s_at_lo, m, 1, 1)
                        bank_read(pe, (s_q_lo, shifted(m, -1)), (s_nbr_in_lo, m), (s_l0_sum, shifted(m, -1)))
                        product(ps_front[1], at, nbr_in).then_inc(s_nbr, 1)
                    if g == 1 and there(i, 1):
                        m = shifted(i, 1)
                        wait_count(pe, s_h2t_lo, m, 1, 1)
                        bank_read(pe, (s_added, shifted(m, -3)),
                                      (s_self_copied, shifted(m, 1)),
                                      (s_v_copied, shifted(m, -1)))
                        product(ps_front[0], h2t, W, first_m=WV).then_inc(s_v, 1)
                    if g == 2 and there(i, -1):
                        m = shifted(i, -1)
                        wait_count(pe, s_attn_copied, m, H, G)
                        wait_count(pe, s_v_copied, m, 1, 1)
                        wait_count(pe, s_ctx_lo, m, 1, 0)
                        if at_start(m, 0):
                            pe.wait_ge(s_bias_copied, 1)
                        context(m, 0).then_inc(s_ctx_half, 1)
                    if g == 4 and there(i, 3):
                        m = shifted(i, 3)
                        if at_start(m, 0):
                            pe.wait_ge(s_w_hi, 1)
                            pe.wait_ge(s_w_lo, 1)
                        wait_count(pe, s_h1t_lo, m, 1, 1)
                        bank_read(pe, (s_l0_sum, shifted(m, -1)),
                                      (s_q_lo, shifted(m, -2)),
                                      (s_nbr_in_lo, shifted(m, -1)))
                        product(ps_front[1], h1t, W, first_m=W0 + T).then_inc(s_nbr_in, 1)
                    if g == 4 and there(i, 2):
                        m = shifted(i, 2)
                        wait_count(pe, s_y2, m, 1, 1)
                        bank_read(pe, (s_h1t_lo, shifted(m, 1)),
                                      (s_k_lo, shifted(m, -1)),
                                      (s_h2t_lo, shifted(m, -1)))
                        transposed(ps_front[2], y2).then_inc(s_y2t, 1)
            run(pe, iteration)

        @block.scalar
        def _(act):
            copy = ACT.Copy

            act.wait_ge(s_weights_first, 16 * 2)
            nc.scalar.activation(w_hi[:, :WQ, :], w_raw[:, :WQ, :], copy).then_inc(s_w_hi, 1)

            def exponentials(i, g):
                p = g % 2
                wait_count(act, s_negmax, i, H, g + 1)
                wait_count(act, s_attn, i, H, g - 1)
                for t in range(T):
                    last = nc.scalar.activation(probs[p][:, t, :], masked[p][:, t, :], ACT.Exp,
                                                bias=neg_max[:, p, t:t + 1], scale=SCALE2,
                                                accum_out=row_sum[:, p, t:t + 1])
                last.then_inc(s_exp, 1)

            def attn_copy(i, g):
                wait_count(act, s_attn_t, i, H, g + 1)
                used = shifted(i, g // H)
                wait_count(act, s_ctx if g % H >= G else s_ctx_half, used, 1, 0)
                nc.scalar.activation(attn_t[:, g % H, :, :], ps_t[g % 2][:, :, :], copy)\
                  .then_inc(s_attn_copied, 1)

            def iteration(i):
                for g in range(H):
                    if head_there(i, g - 4):
                        attn_copy(i, g - 4)
                    if g == 4 and there(i, -1):
                        m = shifted(i, -1)
                        wait_count(act, s_ctx, m, 1, 1)
                        wait_count(act, s_out, m, 1, 0)
                        nc.scalar.activation(ctxt[0][:, :, :], ps_ctx[:, :, :], copy).then_inc(s_ctx_hi, 1)
                    if g == 4 and there(i, 1):
                        m = shifted(i, 1)
                        wait_count(act, s_v, m, 1, 1)
                        wait_count(act, s_ctx, m, 1, -1)
                        nc.scalar.activation(v_sb[m[1] % 2][:, :, :], ps_front[0][:, :, :], copy)\
                          .then_inc(s_v_copied, 1)
                    if g == 6 and there(i, 3):
                        m = shifted(i, 3)
                        wait_count(act, s_self, m, 1, 1)
                        wait_count(act, s_l0_sum, m, 1, 0)
                        nc.scalar.activation(self_part[:, :, :], ps_front[0][:, :, :], copy)\
                          .then_inc(s_self_copied, 1)
                    if g == 7 and there(i, 2):
                        m = shifted(i, 2)
                        wait_count(act, s_k, m, 1, 1)
                        for f in range(T):
                            last = nc.scalar.activation(kq[m[1] % 2][:, K_HI, f, :], ps_front[2][:, f, :],
                                                        ACT.Identity, bias=bk_sb[:, f:f + 1])
                        last.then_inc(s_k_hi, 1)
                    if head_there(i, g):
                        exponentials(i, g)
                    if g == 1 and there(i, 3):
                        m = shifted(i, 3)
                        wait_count(act, s_y1t, m, 1, 1)
                        wait_count(act, s_self, m, 1, 0)
                        nc.scalar.activation(h1t[0][:, :, :], ps_front[2][:, :, :], ACT.Relu)\
                          .then_inc(s_h1t_hi, 1)
                        if at_start(m, 0):
                            act.wait_ge(s_weights, 16 * 7)
                            nc.scalar.activation(w_hi[:, WQ:, :], w_raw[:, WQ:, :], copy).then_inc(s_w_hi, 1)
                    if g == 4 and there(i, 3):
                        m = shifted(i, 3)
                        wait_count(act, s_nbr_in, m, 1, 1)
                        wait_count(act, s_nbr, m, 1, 0)
                        nc.scalar.activation(nbr_in[0][:, :, :], ps_front[1][:, :, :], copy)\
                          .then_inc(s_nbr_in_hi, 1)
                    if g == 4 and there(i, 2):
                        m = shifted(i, 2)
                        wait_count(act, s_y2t, m, 1, 1)
                        wait_count(act, s_v, m, 1, 0)
                        nc.scalar.activation(h2t[0][:, :, :], ps_front[2][:, :, :], ACT.Relu)\
                          .then_inc(s_h2t_hi, 1)
                    if g == 6 and there(i, 2):
                        m = shifted(i, 2)
                        if at_start(m, 0):
                            act.wait_ge(s_bias_ready, 1)
                            nc.scalar.activation(out_bias[:, :], ps_ctx[:, 0, :], copy)\
                              .then_inc(s_bias_copied, 1)
                        wait_count(act, s_q, m, 1, 1)
                        for head in range(G):
                            wait_dma(act, s_stack[head], shifted(m, -2), STACK_INC)
                        for f in range(T):
                            last = nc.scalar.activation(kq[m[1] % 2][:, Q_HI, f, :], ps_front[1][:, f, :],
                                                        ACT.Identity, bias=bq_sb[:, f:f + 1])
                        last.then_inc(s_q_hi, 1)
            run(act, iteration)

        @block.vector
        def _(dve):
            v = nc.vector
            f32 = lambda ap: ap.bitcast(F32)

            def statistics(m, src, stats, mv, s_stats, s_mv):
                for t in range(T):
                    last = v.bn_stats(stats[:, t, :], src[:, t, :])
                last.then_inc(s_stats, 1)
                wait_count(dve, s_stats, m, 1, 1)
                pass_waits(dve, s_passed)
                for t in range(T):
                    last = v.bn_aggr(mv[:, t, :], stats[:, t, :])
                last.then_inc(s_mv, 1)

            def normalised(dst, src, mv, rstd):
                for t in range(T):
                    last = v.tensor_scalar(dst[:, t, :], src[:, t, :], mv[:, t, 0:1], rstd[:, t:t + 1],
                                           ALU.subtract, ALU.mult)
                return last

            def masked_scores(i, g):
                p, m = g % 2, (i[1] + g // H) % 2
                wait_count(dve, s_scores, i, H, g + 1)
                wait_count(dve, s_exp, i, H, g - 1)
                if g % H == 0:
                    wait_dma(dve, s_mask, shifted(i, g // H))
                pass_waits(dve, s_passed)
                for t in range(T):
                    last = v.tensor_tensor_reduce(out=masked[p][:, t, :], in0=ps_s[p][:, t, :], in1=mask[m][:, t, :],
                                                  scale=1.0, scalar=LOWEST, op0=ALU.mult, op1=ALU.max,
                                                  accum_out=row_max[:, p, t:t + 1])
                last.then_inc(s_masked, 1)

            def inverse_sums(i, g):
                p = g % 2
                wait_count(dve, s_exp, i, H, g + 1)
                wait_count(dve, s_attn, i, H, g - 1)
                v.reciprocal(inv_sum[:, p, :], row_sum[:, p, :]).then_inc(s_inv, 1)

            def iteration(i):
                for g in range(H):
                    if head_there(i, g + 1):
                        masked_scores(i, g + 1)
                    if g == 0 and there(i, -2):
                        m = shifted(i, -2)
                        wait_count(dve, s_out, m, 1, 1)
                        wait_count(dve, s_x1_biased, m, 1, 1)
                        wait_dma(dve, s_stored, shifted(m, -2))
                        v.tensor_tensor(out_sb[m[1] % 2][:, :, :], ps_front[0][:, :, :],
                                        x1_biased[m[1] % 2][:, :, :], ALU.add)\
                         .then_inc(s_added, 1)
                    if g == 0 and there(i, 2):
                        m = shifted(i, 2)
                        wait_count(dve, s_deg_inv, m, 1, 1)
                        wait_count(dve, s_nbr, m, 1, 1)
                        wait_count(dve, s_self_copied, m, 1, 1)
                        for t in range(T):
                            last = v.scalar_tensor_tensor(l0_sum[:, t, :], ps_front[1][:, t, :], deg_inv[:, t:t + 1],
                                                          self_part[:, t, :], ALU.mult, ALU.add)
                        last.then_inc(s_l0_sum, 1)
                    if g == 1 and there(i, 2):
                        m = shifted(i, 2)
                        wait_count(dve, s_l0_sum, m, 1, 1)
                        wait_count(dve, s_x1_biased, m, 1, -1)
                        v.scalar_tensor_tensor(x1[m[1] % 2][:, :, :], l0_sum[:, :, :], 0.0, x_sb[m[1] % 2][:, :, :],
                                               ALU.max, ALU.add).then_inc(s_x1, 1)
                    if g == 2 and there(i, 2):
                        m = shifted(i, 2)
                        wait_count(dve, s_x1, m, 1, 1)
                        wait_count(dve, s_rstd2, m, 1, 0)
                        wait_count(dve, s_y2, m, 1, 0)
                        statistics(m, x1[m[1] % 2], stats2, mv2, s_stats2, s_mv2)
                    if g == 2 and there(i, 3):
                        m = shifted(i, 3)
                        if at_start(m, 0):
                            dve.wait_ge(s_weights_first, 16 * 2)
                            v.tensor_copy(bv_wide[:, :, :], bv_sb[:, :].unsqueeze(2).to_broadcast([P, T, P]))\
                              .then_inc(s_bv_wide, 1)
                            dve.wait_ge(s_w_hi, 1)
                            v.tensor_tensor(w_lo[:, :WQ, :], w_raw[:, :WQ, :], f32(w_hi[:, :WQ, :]), ALU.subtract)\
                              .then_inc(s_w_lo, 1)
                        wait_count(dve, s_h1t_hi, m, 1, 1)
                        v.scalar_tensor_tensor(h1t[1][:, :, :], ps_front[2][:, :, :], 0.0, f32(h1t[0][:, :, :]),
                                               ALU.max, ALU.subtract).then_inc(s_h1t_lo, 1)
                    if g == 3 and there(i, 2):
                        m = shifted(i, 2)
                        wait_count(dve, s_rstd2, m, 1, 1)
                        wait_count(dve, s_y2t, m, 1, 0)
                        normalised(y2, x1[m[1] % 2], mv2, rstd2).then_inc(s_y2, 1)
                    if g == 4 and there(i, 4):
                        m = shifted(i, 4)
                        wait_dma(dve, s_x, m)
                        wait_count(dve, s_rstd1, m, 1, 0)
                        wait_count(dve, s_y1, m, 1, 0)
                        statistics(m, x_sb[m[1] % 2], stats1, mv1, s_stats1, s_mv1)
                    if g == 5 and there(i, 3):
                        m = shifted(i, 3)
                        wait_count(dve, s_nbr_in_hi, m, 1, 1)
                        v.tensor_tensor(nbr_in[1][:, :, :], ps_front[1][:, :, :], f32(nbr_in[0][:, :, :]), ALU.subtract)\
                         .then_inc(s_nbr_in_lo, 1)
                        if at_start(m, 0):
                            dve.wait_ge(s_w_hi, 2)
                            v.tensor_tensor(w_lo[:, WQ:, :], w_raw[:, WQ:, :], f32(w_hi[:, WQ:, :]), ALU.subtract)\
                              .then_inc(s_w_lo, 1)
                    if g == 5 and there(i, 2):
                        m = shifted(i, 2)
                        wait_count(dve, s_h2t_hi, m, 1, 1)
                        v.scalar_tensor_tensor(h2t[1][:, :, :], ps_front[2][:, :, :], 0.0, f32(h2t[0][:, :, :]),
                                               ALU.max, ALU.subtract).then_inc(s_h2t_lo, 1)
                    if g == 5 and there(i, -1):
                        m = shifted(i, -1)
                        wait_count(dve, s_ctx_hi, m, 1, 1)
                        v.tensor_tensor(ctxt[1][:, :, :], ps_ctx[:, :, :], f32(ctxt[0][:, :, :]), ALU.subtract)\
                         .then_inc(s_ctx_lo, 1)
                    if g == 5 and there(i, 3):
                        m = shifted(i, 3)
                        wait_dma(dve, s_adjq, m)
                        wait_count(dve, s_deg_max, m, 1, 0)
                        v.tensor_reduce(deg[:, :], adjq_sb[m[1] % 2][:, :, :], axis=mybir.AxisListType.X, op=ALU.add)\
                         .then_inc(s_deg, 1)
                    if g == 6 and there(i, 4):
                        m = shifted(i, 4)
                        wait_count(dve, s_rstd1, m, 1, 1)
                        wait_count(dve, s_y1t, m, 1, 0)
                        normalised(y1, x_sb[m[1] % 2], mv1, rstd1).then_inc(s_y1, 1)
                    if g == 6 and there(i, 3):
                        m = shifted(i, 3)
                        wait_count(dve, s_deg, m, 1, 1)
                        v.tensor_scalar(deg_max[:, :], deg[:, :], DEG_EPS, None, ALU.max).then_inc(s_deg_max, 1)
                        wait_count(dve, s_deg_max, m, 1, 1)
                        wait_count(dve, s_l0_sum, m, 1, 0)
                        v.reciprocal(deg_inv[:, :], deg_max[:, :]).then_inc(s_deg_inv, 1)
                    if g == 7 and there(i, 2):
                        m = shifted(i, 2)
                        wait_count(dve, s_q_hi, m, 1, 1)
                        for f in range(T):
                            last = v.scalar_tensor_tensor(kq[m[1] % 2][:, Q_LO, f, :], ps_front[1][:, f, :], bq_sb[:, f:f + 1],
                                                          f32(kq[m[1] % 2][:, Q_HI, f, :]), ALU.add, ALU.subtract)
                        last.then_inc(s_q_lo, 1)
                        wait_count(dve, s_k_hi, m, 1, 1)
                        for f in range(T):
                            last = v.scalar_tensor_tensor(kq[m[1] % 2][:, K_LO, f, :], ps_front[2][:, f, :], bk_sb[:, f:f + 1],
                                                          f32(kq[m[1] % 2][:, K_HI, f, :]), ALU.add, ALU.subtract)
                        last.then_inc(s_k_lo, 1)
                    if head_there(i, g):
                        inverse_sums(i, g)
            run(dve, iteration)

        @block.gpsimd
        def _(pool):
            gp = nc.gpsimd
            gp.memset(ident[:, :], 0.0).then_inc(s_ident, 1)
            gp.memset(ones_row[:, :], 1.0).then_inc(s_consts, 1)
            gp.memset(minus_half[:, :], -0.5).then_inc(s_consts, 1)
            pool.wait_ge(s_ident, 1)
            gp.affine_select(out=ident[:, :], in_=ident[:, :], compare_op=ALU.not_equal, fill=1.0,
                             base=0, pattern=[[-1, P]], channel_multiplier=1).then_inc(s_ident, 1)
            pool.wait_ge(s_consts, 2)

            def negative_maxima(i, g):
                p = g % 2
                wait_count(pool, s_masked, i, H, g + 1)
                pass_waits(pool, s_passed)
                gp.tensor_scalar(neg_max[:, p, :], row_max[:, p, :], -SCALE2, 0.0, ALU.mult, ALU.add)\
                  .then_inc(s_negmax, 1)

            def normalised_attention(i, g):
                p = g % 2
                wait_count(pool, s_inv, i, H, g + 1)
                wait_count(pool, s_attn_t, i, H, g - 1)
                pass_waits(pool, s_passed)
                for t in range(T):
                    last = gp.tensor_scalar(attn[p][:, t, :], probs[p][:, t, :], inv_sum[:, p, t:t + 1], 0.0,
                                            ALU.mult, ALU.add)
                last.then_inc(s_attn, 1)

            def iteration(i):
                for g in range(H):
                    if g == 3 and there(i, 3):
                        m = shifted(i, 3)
                        wait_dma(pool, s_adjt, m)
                        wait_count(pool, s_nbr, m, 1, 0)
                        pass_waits(pool, s_passed)
                        gp.tensor_scalar(at[0][:, :, :], adjt_sb[m[1] % 2][:, :, :], 1.0, 0.0, ALU.mult, ALU.add)\
                          .then_inc(s_at_hi, 1)
                    if g == 4 and there(i, 2):
                        m = shifted(i, 2)
                        wait_count(pool, s_mv2, m, 1, 1)
                        wait_count(pool, s_y2, m, 1, 0)
                        pass_waits(pool, s_passed)
                        gp.tensor_scalar(var2[:, :], mv2[:, :, 1], LN_EPS, 0.0, ALU.add, ALU.add)\
                          .then_inc(s_var2, 1)
                        wait_count(pool, s_var2, m, 1, 1)
                        gp.tensor_tensor(rstd2[:, :], var2[:, :], minus_half[:, :], ALU.pow)\
                          .then_inc(s_rstd2, 1)
                    if g == 5 and there(i, 3):
                        m = shifted(i, 3)
                        wait_count(pool, s_at_hi, m, 1, 1)
                        gp.tensor_tensor(at[1][:, :, :], adjt_sb[m[1] % 2][:, :, :], at[0][:, :, :].bitcast(F32),
                                         ALU.subtract).then_inc(s_at_lo, 1)
                    if head_there(i, g - 2):
                        normalised_attention(i, g - 2)
                    if head_there(i, g):
                        negative_maxima(i, g)
                    if g == 1 and there(i):
                        m = i
                        wait_count(pool, s_x1, m, 1, 1)
                        wait_count(pool, s_added, m, 1, -1)
                        if at_start(m, 0):
                            pool.wait_ge(s_bias_copied, 1)
                        gp.tensor_tensor(x1_biased[m[1] % 2][:, :, :], x1[m[1] % 2][:, :, :],
                                         out_bias[:, :].unsqueeze(1).to_broadcast([P, T, F]), ALU.add)\
                                           .then_inc(s_x1_biased, 1)
                    if g == 6 and there(i, 4):
                        m = shifted(i, 4)
                        wait_count(pool, s_mv1, m, 1, 1)
                        wait_count(pool, s_y1, m, 1, 0)
                        pass_waits(pool, s_passed)
                        gp.tensor_scalar(var1[:, :], mv1[:, :, 1], LN_EPS, 0.0, ALU.add, ALU.add)\
                          .then_inc(s_var1, 1)
                        wait_count(pool, s_var1, m, 1, 1)
                        gp.tensor_tensor(rstd1[:, :], var1[:, :], minus_half[:, :], ALU.pow)\
                          .then_inc(s_rstd1, 1)
            run(pool, iteration)


def kernel(x, adj, L0_gnn_W, L1_gnn_Wq, L1_gnn_bq, L1_gnn_Wk, L1_gnn_bk, L1_gnn_Wv, L1_gnn_bv, L1_gnn_Wo, L1_gnn_bo):
    import numpy as np
    import concourse.bacc as bacc
    from concourse.bass_utils import run_bass_kernel_spmd

    x, adj = np.asarray(x), np.asarray(adj)
    B = x.shape[0]

    def weight(w):
        w = np.asarray(w)
        return np.ascontiguousarray(w.T.reshape(-1, P, w.shape[0]).transpose(1, 0, 2))

    def column(v):
        return np.ascontiguousarray(np.asarray(v).reshape(T, P).T)

    a = adj.reshape(B, P, T, P, T)
    arrays = {
        "x": np.ascontiguousarray(x.reshape(B, P, T, F)),
        "adjq": np.ascontiguousarray(a.transpose(0, 1, 2, 4, 3)).reshape(B, P, T, N),
        "adjt": np.ascontiguousarray(a.transpose(0, 3, 4, 2, 1)).reshape(B, P, T, N),
        "w0": weight(L0_gnn_W),
        "wq": weight(L1_gnn_Wq),
        "wk": weight(L1_gnn_Wk),
        "wv": weight(L1_gnn_Wv),
        "wo": weight(L1_gnn_Wo),
        "bq": column(L1_gnn_bq),
        "bk": column(L1_gnn_bk),
        "bv": column(L1_gnn_bv),
        "bo": np.ascontiguousarray(np.asarray(L1_gnn_bo).reshape(1, F)),
    }
    nc = bacc.Bacc("TRN2", target_bir_lowering=False, num_devices=1)
    ins = [nc.dram_tensor(name, v.shape, mybir.dt.from_np(v.dtype), kind="ExternalInput").ap()
           for name, v in arrays.items()]
    out = nc.dram_tensor("out", (B, P, T, F), F32, kind="ExternalOutput").ap()
    build(nc, *ins, out)
    r = run_bass_kernel_spmd(nc, [arrays], core_ids=[0])
    return r.results[0]["out"].reshape(B, N, F)
```
